# Optimizing a Trainium2 kernel written in Bass

```python
import numpy as np
import jax
import jax.numpy as jnp

def _softmax(x, axis=-1):
    return jax.nn.softmax(x, axis=axis)

def _gelu(x):
    return jax.nn.gelu(x, approximate=True)

def _silu(x):
    return jax.nn.silu(x)

def _sigmoid(x):
    return jax.nn.sigmoid(x)

def _layernorm(x, axis=-1, eps=1e-05):
    m = jnp.mean(x, axis=axis, keepdims=True)
    v = jnp.var(x, axis=axis, keepdims=True)
    return (x - m) / jnp.sqrt(v + eps)

def _scatter_add(tgt, idx, src, axis=0):
    return tgt.at[idx].add(src)

def _segment_sum(src, seg, n):
    return jax.ops.segment_sum(src, seg, n)
kernel_name = 'mk_gnn_preln_d4_gnn_r8_776d1c'

def setup_inputs(seed: int=0):
    np.random.seed(seed)
    _w = jnp.asarray

    def _rec_inputs():
        import jax
        import jax.numpy as jnp
        _gk = jax.random.key(seed)
        x = -0.000202 + 1 * jax.random.normal(jax.random.fold_in(_gk, 1), (12500, 128), jnp.float32)
        src = jax.random.randint(jax.random.fold_in(_gk, 2), (200000,), 0, 12500, jnp.int32)
        dst = jax.random.randint(jax.random.fold_in(_gk, 3), (200000,), 0, 12500, jnp.int32)
        _o = jnp.argsort(dst, stable=True)
        src = src[_o]
        dst = dst[_o]
        edge_attr_128 = jax.random.uniform(jax.random.fold_in(_gk, 12), (200000, 128), jnp.float32, 0.0, 1)
        edge_attr_3 = -0.000451519 + 1.00018 * jax.random.normal(jax.random.fold_in(_gk, 13), (200000, 3), jnp.float32)
        edge_type_8 = jax.random.randint(jax.random.fold_in(_gk, 14), (200000,), 0, 8, jnp.int32)
        edge_weight = jax.random.uniform(jax.random.fold_in(_gk, 15), (200000,), jnp.float32, 0.0, 1)
        return (x, src, dst, edge_attr_128, edge_attr_3, edge_type_8, edge_weight)
    x, src, dst, edge_attr_128, edge_attr_3, edge_type_8, edge_weight = _rec_inputs()

    def _L0_gnn_setup():
        import jax, jax.numpy as jnp
        import numpy as np
        N_NODES = 6250
        N_EDGES = 100000
        N_RELS = 8
        N_BASES = 4
        IN_FEAT = 128
        OUT_FEAT = 128
        key = jax.random.key(seed)
        k = jax.random.split(key, 7)
        x = jax.random.normal(k[0], (N_NODES, IN_FEAT), dtype=jnp.float32)
        edge_norm = jax.random.uniform(k[1], (N_EDGES,), dtype=jnp.float32)
        bases = jax.random.normal(k[2], (N_BASES, IN_FEAT, OUT_FEAT), dtype=jnp.float32) * 0.05
        w_comp = jax.random.normal(k[3], (N_RELS, N_BASES), dtype=jnp.float32)
        edge_src = jax.random.randint(k[4], (N_EDGES,), 0, N_NODES, dtype=jnp.int32)
        edge_dst = jax.random.randint(k[5], (N_EDGES,), 0, N_NODES, dtype=jnp.int32)
        edge_type = jax.random.randint(k[6], (N_EDGES,), 0, N_RELS, dtype=jnp.int32)
        return {'x': x, 'edge_norm': edge_norm, 'bases': bases, 'w_comp': w_comp, 'edge_src': edge_src, 'edge_dst': edge_dst, 'edge_type': edge_type}
    _L0_gnn_all = _L0_gnn_setup()
    _L0_gnn_in = {k: v for k, v in _L0_gnn_all.items() if k in ('bases', 'w_comp')}
    del _L0_gnn_all

    def _L1_gnn_setup():
        import jax, jax.numpy as jnp
        import numpy as np
        N = 6250
        E = 100000
        MUL = 32
        NB = 8
        R_MAX = 1.0
        AVG = 16.0
        SQ3 = 3.0 ** 0.5

        def _radial_embedding(r):
            x = jnp.clip(r / R_MAX, 0.0, 1.0)
            centers = jnp.arange(NB, dtype=jnp.float32) / (NB - 1)
            sigma = 1.0 / (NB - 1)
            emb = jnp.exp(-0.5 * ((x[:, None] - centers[None, :]) / sigma) ** 2)
            emb = emb * NB ** 0.5 * (r <= R_MAX).astype(jnp.float32)[:, None]
            return emb
        key = jax.random.key(seed)
        k = jax.random.split(key, 12)
        inp = {'node_feats': jax.random.normal(k[0], (N, 4 * MUL), dtype=jnp.float32), 'edge_vec': jax.random.normal(k[1], (E, 3), dtype=jnp.float32), 'edge_length': jax.random.uniform(k[2], (E,), dtype=jnp.float32), 'senders': jax.random.randint(k[3], (E,), 0, N, dtype=jnp.int32), 'receivers': jax.random.randint(k[4], (E,), 0, N, dtype=jnp.int32), 'num_nodes': N, 'W_up0': jax.random.normal(k[5], (MUL, MUL), dtype=jnp.float32), 'W_up1': jax.random.normal(k[6], (MUL, MUL), dtype=jnp.float32), 'mlp_w0': jax.random.normal(k[7], (NB, 64), dtype=jnp.float32) / NB ** 0.5, 'mlp_b0': jnp.zeros((64,), dtype=jnp.float32), 'mlp_w1': jax.random.normal(k[8], (64, 64), dtype=jnp.float32) / 8.0, 'mlp_b1': jnp.zeros((64,), dtype=jnp.float32), 'mlp_w2': jax.random.normal(k[9], (64, 4 * MUL), dtype=jnp.float32) / 8.0, 'mlp_b2': jnp.zeros((4 * MUL,), dtype=jnp.float32), 'W_out0': jax.random.normal(k[10], (2 * MUL, MUL), dtype=jnp.float32), 'W_out1': jax.random.normal(k[11], (2 * MUL, MUL), dtype=jnp.float32)}
        return inp
    _L1_gnn_all = _L1_gnn_setup()
    _L1_gnn_in = {k: v for k, v in _L1_gnn_all.items() if k in ('W_up0', 'W_up1', 'mlp_w0', 'mlp_b0', 'mlp_w1', 'mlp_b1', 'mlp_w2', 'mlp_b2', 'W_out0', 'W_out1')}
    del _L1_gnn_all

    def _L2_gnn_setup():
        import jax, jax.numpy as jnp
        import numpy as np
        N_NODES = 6250
        N_EDGES = 75000
        DIM = 128
        key = jax.random.key(seed)
        ks = jax.random.split(key, 10)
        s = 1.0 / np.sqrt(DIM)
        return {'x': jax.random.normal(ks[0], (N_NODES, DIM), dtype=jnp.float32), 'i': jax.random.randint(ks[1], (N_EDGES,), 0, N_NODES), 'j': jax.random.randint(ks[2], (N_EDGES,), 0, N_NODES), 'rbf': jax.random.uniform(ks[3], (N_EDGES, DIM), dtype=jnp.float32), 'Wl': jax.random.normal(ks[4], (DIM, DIM), dtype=jnp.float32) * s, 'bl': jnp.zeros((DIM,), dtype=jnp.float32), 'W0': jax.random.normal(ks[5], (DIM, DIM), dtype=jnp.float32) * s, 'b0': jnp.zeros((DIM,), dtype=jnp.float32), 'W2': jax.random.normal(ks[6], (DIM, DIM), dtype=jnp.float32) * s, 'b2': jnp.zeros((DIM,), dtype=jnp.float32), 'gamma': jnp.ones((DIM,), dtype=jnp.float32), 'beta': jnp.zeros((DIM,), dtype=jnp.float32)}
    _L2_gnn_all = _L2_gnn_setup()
    _L2_gnn_in = {k: v for k, v in _L2_gnn_all.items() if k in ('Wl', 'bl', 'W0', 'b0', 'W2', 'b2', 'gamma', 'beta')}
    del _L2_gnn_all

    def _L3_gnn_setup():
        import jax, jax.numpy as jnp
        import numpy as np
        N_NODES = 6250
        N_EDGES = 75000
        D = 128

        def _graph_conv(h, src, dst, norm_src, norm_dst, W, b):
            m = (h * norm_src[:, None])[src]
            agg = jnp.zeros_like(h).at[dst].add(m)
            agg = agg * norm_dst[:, None]
            return jax.nn.relu(agg @ W + b)
        key = jax.random.key(seed)
        ks = jax.random.split(key, 5)
        features = jax.random.normal(ks[0], (N_NODES, D), dtype=jnp.float32)
        src = jax.random.randint(ks[1], (N_EDGES,), 0, N_NODES, dtype=jnp.int64)
        dst = jax.random.randint(ks[2], (N_EDGES,), 0, N_NODES, dtype=jnp.int64)
        W1 = jax.random.normal(ks[3], (D, D), dtype=jnp.float32) / np.sqrt(D)
        W2 = jax.random.normal(ks[4], (D, D), dtype=jnp.float32) / np.sqrt(D)
        b1 = jnp.zeros((D,), dtype=jnp.float32)
        b2 = jnp.zeros((D,), dtype=jnp.float32)
        return {'features': features, 'src': src, 'dst': dst, 'W1': W1, 'b1': b1, 'W2': W2, 'b2': b2}
    _L3_gnn_all = _L3_gnn_setup()
    _L3_gnn_in = {k: v for k, v in _L3_gnn_all.items() if k in ('W1', 'b1', 'W2', 'b2')}
    del _L3_gnn_all
    return {'x': x, 'src': src, 'dst': dst, 'edge_attr_128': edge_attr_128, 'edge_attr_3': edge_attr_3, 'edge_type_8': edge_type_8, 'edge_weight': edge_weight, 'L0_gnn_bases': _L0_gnn_in['bases'], 'L0_gnn_w_comp': _L0_gnn_in['w_comp'], 'L1_gnn_W_up0': _L1_gnn_in['W_up0'], 'L1_gnn_W_up1': _L1_gnn_in['W_up1'], 'L1_gnn_mlp_w0': _L1_gnn_in['mlp_w0'], 'L1_gnn_mlp_b0': _L1_gnn_in['mlp_b0'], 'L1_gnn_mlp_w1': _L1_gnn_in['mlp_w1'], 'L1_gnn_mlp_b1': _L1_gnn_in['mlp_b1'], 'L1_gnn_mlp_w2': _L1_gnn_in['mlp_w2'], 'L1_gnn_mlp_b2': _L1_gnn_in['mlp_b2'], 'L1_gnn_W_out0': _L1_gnn_in['W_out0'], 'L1_gnn_W_out1': _L1_gnn_in['W_out1'], 'L2_gnn_Wl': _L2_gnn_in['Wl'], 'L2_gnn_bl': _L2_gnn_in['bl'], 'L2_gnn_W0': _L2_gnn_in['W0'], 'L2_gnn_b0': _L2_gnn_in['b0'], 'L2_gnn_W2': _L2_gnn_in['W2'], 'L2_gnn_b2': _L2_gnn_in['b2'], 'L2_gnn_gamma': _L2_gnn_in['gamma'], 'L2_gnn_beta': _L2_gnn_in['beta'], 'L3_gnn_W1': _L3_gnn_in['W1'], 'L3_gnn_b1': _L3_gnn_in['b1'], 'L3_gnn_W2': _L3_gnn_in['W2'], 'L3_gnn_b2': _L3_gnn_in['b2']}

def reference(x, src, dst, edge_attr_128, edge_attr_3, edge_type_8, edge_weight, L0_gnn_bases, L0_gnn_w_comp, L1_gnn_W_up0, L1_gnn_W_up1, L1_gnn_mlp_w0, L1_gnn_mlp_b0, L1_gnn_mlp_w1, L1_gnn_mlp_b1, L1_gnn_mlp_w2, L1_gnn_mlp_b2, L1_gnn_W_out0, L1_gnn_W_out1, L2_gnn_Wl, L2_gnn_bl, L2_gnn_W0, L2_gnn_b0, L2_gnn_W2, L2_gnn_b2, L2_gnn_gamma, L2_gnn_beta, L3_gnn_W1, L3_gnn_b1, L3_gnn_W2, L3_gnn_b2):
    import jax
    import jax.numpy as jnp

    def _L0_gnn_ref(x, edge_norm, bases, w_comp, edge_src, edge_dst, edge_type):
        import jax, jax.numpy as jnp
        import numpy as np
        N_NODES = 6250
        N_EDGES = 100000
        N_RELS = 8
        N_BASES = 4
        IN_FEAT = 128
        OUT_FEAT = 128
        N = x.shape[0]
        R = w_comp.shape[0]
        W = jnp.einsum('rb,bio->rio', w_comp, bases)
        msg = x[edge_src] * edge_norm[:, None]
        seg = edge_type * N + edge_dst
        agg = jax.ops.segment_sum(msg, seg, num_segments=R * N)
        agg = agg.reshape(R, N, -1)
        out = jnp.einsum('rni,rio->no', agg, W)
        return out

    def _L1_gnn_ref(node_feats, edge_vec, edge_length, senders, receivers, num_nodes, W_up0, W_up1, mlp_w0, mlp_b0, mlp_w1, mlp_b1, mlp_w2, mlp_b2, W_out0, W_out1):
        import jax, jax.numpy as jnp
        import numpy as np
        N = 6250
        E = 100000
        MUL = 32
        NB = 8
        R_MAX = 1.0
        AVG = 16.0
        SQ3 = 3.0 ** 0.5

        def _radial_embedding(r):
            x = jnp.clip(r / R_MAX, 0.0, 1.0)
            centers = jnp.arange(NB, dtype=jnp.float32) / (NB - 1)
            sigma = 1.0 / (NB - 1)
            emb = jnp.exp(-0.5 * ((x[:, None] - centers[None, :]) / sigma) ** 2)
            emb = emb * NB ** 0.5 * (r <= R_MAX).astype(jnp.float32)[:, None]
            return emb
        f32 = jnp.float32
        rhat = edge_vec / (jnp.linalg.norm(edge_vec, axis=-1, keepdims=True) + 1e-12)
        Y1 = SQ3 * rhat
        emb = _radial_embedding(edge_length)
        h = jax.nn.silu(emb @ mlp_w0 + mlp_b0)
        h = jax.nn.silu(h @ mlp_w1 + mlp_b1)
        w = (h @ mlp_w2 + mlp_b2).reshape(-1, 4, MUL)
        s = node_feats[:, :MUL]
        v = node_feats[:, MUL:].reshape(-1, MUL, 3)
        xs = s @ W_up0 / f32(MUL) ** 0.5
        xv = jnp.einsum('nmc,mk->nkc', v, W_up1) / f32(MUL) ** 0.5
        ss = xs[senders]
        vv = xv[senders]
        m0 = w[:, 0] * ss
        m1 = w[:, 1][:, :, None] * ss[:, :, None] * Y1[:, None, :]
        m2 = w[:, 2][:, :, None] * vv
        m3 = w[:, 3] * (jnp.einsum('emc,ec->em', vv, Y1) / SQ3)
        mid_s = jnp.concatenate([m0, m3], axis=1)
        mid_v = jnp.concatenate([m1, m2], axis=1)
        msg_s = jax.ops.segment_sum(mid_s, receivers, num_segments=num_nodes)
        msg_v = jax.ops.segment_sum(mid_v, receivers, num_segments=num_nodes)
        out_s = msg_s @ W_out0 / f32(2 * MUL) ** 0.5
        out_v = jnp.einsum('nmc,mk->nkc', msg_v, W_out1) / f32(2 * MUL) ** 0.5
        out = jnp.concatenate([out_s, out_v.reshape(-1, 3 * MUL)], axis=1)
        return out / max(AVG, 1e-08)

    def _L2_gnn_ref(x, i, j, rbf, Wl, bl, W0, b0, W2, b2, gamma, beta):
        import jax, jax.numpy as jnp
        import numpy as np
        N_NODES = 6250
        N_EDGES = 75000
        DIM = 128
        Wxh = x @ Wl.T + bl
        m = rbf @ W0.T
        m = jax.nn.silu(m @ W0.T + b0) @ W2.T + b2
        msg = m * Wxh[j]
        agg = jax.ops.segment_sum(msg, i, num_segments=x.shape[0])
        h = x + agg
        mu = jnp.mean(h, axis=-1, keepdims=True)
        var = jnp.mean(jnp.square(h - mu), axis=-1, keepdims=True)
        return (h - mu) / jnp.sqrt(var + 1e-05) * gamma + beta

    def _L3_gnn_ref(features, src, dst, W1, b1, W2, b2):
        import jax, jax.numpy as jnp
        import numpy as np
        N_NODES = 6250
        N_EDGES = 75000
        D = 128

        def _graph_conv(h, src, dst, norm_src, norm_dst, W, b):
            m = (h * norm_src[:, None])[src]
            agg = jnp.zeros_like(h).at[dst].add(m)
            agg = agg * norm_dst[:, None]
            return jax.nn.relu(agg @ W + b)
        N = features.shape[0]
        ones = jnp.ones(src.shape[0], dtype=features.dtype)
        deg_out = jnp.zeros(N, dtype=features.dtype).at[src].add(ones)
        deg_in = jnp.zeros(N, dtype=features.dtype).at[dst].add(ones)
        norm_src = jax.lax.rsqrt(jnp.clip(deg_out, 1.0))
        norm_dst = jax.lax.rsqrt(jnp.clip(deg_in, 1.0))
        h = _graph_conv(features, src, dst, norm_src, norm_dst, W1, b1) + features
        h = _graph_conv(h, src, dst, norm_src, norm_dst, W2, b2) + features
        return h + features
    h = jnp.maximum(_layernorm(x, axis=-1), 0.0)
    x = x + _L0_gnn_ref(h, edge_weight, L0_gnn_bases, L0_gnn_w_comp, src, dst, edge_type_8)
    h = jnp.maximum(_layernorm(x, axis=-1), 0.0)
    x = x + _L1_gnn_ref(h, edge_attr_3, edge_weight, src, dst, 12500, L1_gnn_W_up0, L1_gnn_W_up1, L1_gnn_mlp_w0, L1_gnn_mlp_b0, L1_gnn_mlp_w1, L1_gnn_mlp_b1, L1_gnn_mlp_w2, L1_gnn_mlp_b2, L1_gnn_W_out0, L1_gnn_W_out1)
    h = jnp.maximum(_layernorm(x, axis=-1), 0.0)
    x = x + _L2_gnn_ref(h, src, dst, edge_attr_128, L2_gnn_Wl, L2_gnn_bl, L2_gnn_W0, L2_gnn_b0, L2_gnn_W2, L2_gnn_b2, L2_gnn_gamma, L2_gnn_beta)
    h = jnp.maximum(_layernorm(x, axis=-1), 0.0)
    x = x + _L3_gnn_ref(h, src, dst, L3_gnn_W1, L3_gnn_b1, L3_gnn_W2, L3_gnn_b2)
    return x

_drawn_inputs = setup_inputs


def setup_inputs(seed=0):
    import zlib

    import numpy as np

    out = dict(_drawn_inputs(seed))
    spreads = {'L1_gnn_mlp_b0': (0.0, 0.8),
     'L1_gnn_mlp_b1': (0.0, 0.8),
     'L1_gnn_mlp_b2': (0.0, 0.59),
     'L2_gnn_bl': (0.0, 0.1),
     'L2_gnn_b0': (0.0, 0.1),
     'L2_gnn_b2': (0.0, 0.1),
     'L2_gnn_gamma': (1.0, 0.2),
     'L2_gnn_beta': (0.0, 0.267),
     'L3_gnn_b1': (0.0, 0.794),
     'L3_gnn_b2': (0.0, 0.534)}
    factors = {'edge_attr_3': 3.477, 'L1_gnn_W_up0': 2.765, 'L1_gnn_W_out0': 3.296}
    for name, (base, spread) in spreads.items():
        noise = np.random.default_rng([zlib.crc32(name.encode()), seed]).standard_normal(out[name].shape)
        drawn = base * np.exp(spread * noise) if base else spread * noise
        out[name] = jnp.asarray(drawn.astype(out[name].dtype))
    for name, factor in factors.items():
        out[name] = (out[name] * factor).astype(out[name].dtype)
    return out
```

```python
import concourse.bass as bass
from concourse import mybir
from contextlib import ExitStack

P = 128
NODES = 12500
EDGES = 200000
FEAT = 128
RELS = 8
BASES = 4
MUL = 32
CENTERS = 8
GT = 8
IG = 4
IT = GT * IG
ITS = -(-EDGES // (P * IT))
GROUPS = ITS * IG
TILES = GROUPS * GT
W = 80
UNITS = 25
NB = 4 * UNITS
NP = NB * P
KV = -(-NP // W)
ADDR_MAX = NP - W
EPS = 1e-5
COPIES = 4
SPARE = NP - P
LIN = GROUPS // 2
LASTU = 2 * UNITS

RES = dict(wup=128, woa=128, wob=128, ew=IG * 128, w1b=128, w2p=256, w2t=128, wlt=128,
           bl=128, gamma=128, beta=128, g1=128, g2=128, gb1=128, gb2=128,
           ident=128, mb0=1, mb1=1, cb0=1, ncen=1, rowm=3, rowno=1, eps=1)
EARLY = dict(bases=BASES * 128, wcomp=RELS * BASES, w0=128, w0t=128, b2a=128, b2b=128, kvec=KV, iota=128, before=128)


def offsets(table):
    at, out = 0, {}
    for name, n in table.items():
        out[name] = (at, at + n)
        at += n
    return out, at


RES_AT, RES_N = offsets(RES)
EARLY_AT, EARLY_N = offsets(EARLY)
EARLY_FROM = 5120


def gnn_kernel(nc, x, src, dst, srcl, dstl, etype, eweight, radii, evec, rbf, resident, early, out):
    fp32 = mybir.dt.float32
    bf16 = mybir.dt.bfloat16
    i32 = mybir.dt.int32
    ALU = mybir.AluOpType
    ACT = mybir.ActivationFunctionType
    AX = mybir.AxisListType
    MAX = bass.bass_isa.ReduceOp.max
    ds = bass.ds

    tab0 = nc.dram_tensor("tab0", [NP * RELS, FEAT], fp32).ap()
    tabs = [tab0] + [nc.dram_tensor(f"tab{p}", [NP, FEAT], fp32).ap() for p in range(1, 5)]
    idx0 = nc.dram_tensor("idx0", [ITS, P, IT], i32).ap()
    emb_d = nc.dram_tensor("emb_d", [2 * UNITS, 64, 512], fp32).ap()
    y_d = nc.dram_tensor("y_d", [ITS, P, 3 * IT], fp32).ap()
    i16 = mybir.dt.int16
    srow_d = nc.dram_tensor("srow_d", [GROUPS, GT * P], i16).ap()
    drow_d = nc.dram_tensor("drow_d", [GROUPS, GT * P], i16).ap()
    sidx = nc.dram_tensor("sidx", [ITS, P, IT], i32).ap()
    accs = [nc.dram_tensor(f"acc{c}", [NP, FEAT], fp32).ap() for c in range(COPIES)]

    ctx = ExitStack()
    with ctx:
        def sb(name, shape, dt=fp32):
            return ctx.enter_context(nc.sbuf_tensor(name, shape, dt))

        def sem(name):
            return ctx.enter_context(nc.semaphore(name))

        X = sb("X", [P, NB, FEAT])
        A0 = sb("A0", [P, NP])
        A1 = sb("A1", [P, NP])
        WORK = sb("WORK", [P, 9568])
        R = sb("R", [P, RES_N])
        DREL = sb("DREL", [P, TILES])
        CW = sb("CW", [P, 128])
        B2S = sb("B2S", [P, 2, 128], bf16)
        ONES = sb("ONES", [P, 128], bf16)
        IOB = sb("IOB", [P, 128], bf16)
        IDX = sb("IDX", [P, 2, IT // 2], i32)
        DEG = sb("DEG", [P, 2, NB])
        ADDR0 = sb("ADDR0", [1, GROUPS], i32)
        ADDR = sb("ADDR", [1, GROUPS], i32)
        NRI = sb("NRI", [1, 1], i32)
        NRW = sb("NRW", [P, 1])
        NODE = sb("NODE", [P, 1])
        BANK = [ctx.enter_context(nc.psum_tensor(f"BANK{b}", [P, 512], fp32)) for b in range(8)]

        def res(name, rows=P):
            a, b = RES_AT[name]
            return R[0:rows, a:b]

        def work(at, n, rows=P):
            return WORK[0:rows, at:at + n]

        def early_w(name, rows=P):
            a, b = EARLY_AT[name]
            return work(EARLY_FROM + a, b - a, rows)

        ring = work(0, 4096).rearrange("p (g t f) -> p g t f", g=IG, t=GT)
        sel = work(4096, 2 * GT * W).rearrange("p (s t w) -> p s t w", s=2, t=GT)
        oh = work(5376, GT * 114).bitcast(bf16).rearrange("p (t n) -> p t n", t=GT)
        msg1 = work(5376, 2048).rearrange("p (s t f) -> p s t f", s=2, t=4)
        h1 = work(7424, 512)
        h2 = work(7936, 512)
        emb = work(8448, 512)
        scals = work(8960, 256).rearrange("p (s t m) -> p s t m", s=2, t=4)
        ubufs = work(9216, 256).rearrange("p (s t m) -> p s t m", s=2, t=4)
        ybuf = work(9472, 96).rearrange("p (h t c) -> p h t c", h=2, c=3)
        srow0 = work(7200, 1024).bitcast(i16).rearrange("p (s n) -> p s n", s=2)
        same0 = work(8224, 512).bitcast(bf16).rearrange("p (t e) -> p t e", t=GT)
        dsts_i = work(4096, TILES).bitcast(i32)
        dpart_i = work(4096 + TILES, TILES).bitcast(i32)
        dst_bits = work(4096 + 2 * TILES, TILES).bitcast(bf16).rearrange("p (k n) -> p k n", k=2)
        rbf_t = A0[:, 0:2048].rearrange("p (s n) -> p s n", s=2)
        srow = A0[:, 2048:3072].bitcast(i16).rearrange("p (s n) -> p s n", s=2)
        drow = A0[:, 3072:4096].bitcast(i16).rearrange("p (s n) -> p s n", s=2)
        twin = A0[:, 4096:4352].rearrange("p (s f) -> p s f", s=2)
        pick = A0[:, 4352:6400].rearrange("p (s n) -> p s n", s=2)
        same = A0[:, 6400:8448].rearrange("p (s t e) -> p s t e", s=2, t=GT)
        hs2 = A0[:, 8448:9472].rearrange("p (s n) -> p s n", s=2)
        mout = A0[:, 9472:10496].rearrange("p (s n) -> p s n", s=2)
        msg2 = A0[:, 10496:11520].rearrange("p (s t f) -> p s t f", s=2, t=4)
        srcc = A0[:, 11520:11552].bitcast(i32)
        parts = A0[:, 0:2048].rearrange("p (s c n) -> p s c n", s=2, c=COPIES)
        stage = work(0, 1024).rearrange("p (s a n) -> p s a n", s=2, a=2)
        hrow = work(1024, 512).rearrange("p (s b f) -> p s b f", s=2, b=2)
        hT = work(1536, 512).rearrange("p (s b f) -> p s b f", s=2, b=2)
        trow = work(2048, 512).rearrange("p (s b f) -> p s b f", s=2, b=2)
        stat = work(2560, 6 * NB).rearrange("p (b c) -> p b c", c=6)
        rstd = work(3160, NB)
        nmr = work(3260, NB)
        mean = work(3360, NB)
        var = work(3460, NB)
        dif = work(3560, NB)
        t0row = work(6656, 2048).rearrange("p (s n) -> p s n", s=2)
        wall = work(3712, RELS * 128)
        gmin = work(8704, GROUPS)
        base = work(8900, GROUPS)
        dmax = work(9096, 2)
        kcmp = work(9100, KV)
        b2f = work(9264, 128)

        A1b = A1[:, :].bitcast(bf16)
        dst_i = A0[:, 0:TILES].bitcast(i32)
        src_i = A0[:, TILES:2 * TILES].bitcast(i32)
        typ_i = A0[:, 2 * TILES:3 * TILES].bitcast(i32)
        idx_i = A0[:, 3 * TILES:4 * TILES].bitcast(i32)
        vec = A1[:, 0:3 * TILES].rearrange("p (t c) -> p t c", c=3)
        vsq = A1[:, 3 * TILES:6 * TILES].rearrange("p (t c) -> p t c", c=3)
        vlen = A1[:, 6 * TILES:7 * TILES]
        ew_t = A1[:, 0:TILES]
        src_bits = A1b[:, 2 * TILES:4 * TILES].rearrange("p (k n) -> p k n", k=2)
        srcs_i = A1[:, 3 * TILES:4 * TILES].bitcast(i32)
        part_i = A1[:, 5 * TILES:6 * TILES].bitcast(i32)
        earlier = A1[:, 5 * TILES:6 * TILES]
        sidx_f = A1[:, 6 * TILES:7 * TILES]
        sidx_i = A1[:, 7 * TILES:8 * TILES].bitcast(i32)
        beforeb = A1b[:, 25088:25088 + 128]
        dstl_i = A0[0:LIN, 4 * TILES:4 * TILES + 2048].bitcast(i32)
        srcl_i = A0[0:LIN, 4 * TILES + 2048:4 * TILES + 4096].bitcast(i32)
        low = A0[0:LIN, 4 * TILES + 4096:4 * TILES + 4098]
        dstl_s = A0[0:LIN, 11000:11000 + 1024].bitcast(i16)
        srcl_s = X[0:LIN, 90:98, :].rearrange("p b f -> p (b f)").bitcast(i16)

        s_res = sem("s_res")
        s_early = sem("s_early")
        s_x = [sem(f"s_x{c}") for c in range(4)]
        s_dst, s_src, s_typ = sem("s_dst"), sem("s_src"), sem("s_typ")
        s_vec, s_rad, s_ewt, s_srcs, s_dsts = (sem(n) for n in ("s_vec", "s_rad", "s_ewt", "s_srcs", "s_dsts"))
        s_idxc, s_idx0, s_ystored, s_emb = (sem(n) for n in ("s_idxc", "s_idx0", "s_ystored", "s_emb"))
        chain = sem("chain")
        s_gmin, s_gall, s_dmax, s_dall, s_nr = (sem(n) for n in ("s_gmin", "s_gall", "s_dmax", "s_dall", "s_nr"))
        s_cmm, s_cok, s_wall, s_ysum, s_ysq, s_y = (sem(n) for n in ("s_cmm", "s_cok", "s_wall", "s_ysum", "s_ysq", "s_y"))
        s_clip, s_sq, s_exp, s_embok, s_ew = (sem(n) for n in ("s_clip", "s_sq", "s_exp", "s_embok", "s_ew"))
        s_zero0 = [sem(f"s_zero0{p}") for p in range(5)]
        s_zero1 = sem("s_zero1")
        s_deg, s_degr = sem("s_deg"), sem("s_degr")

        GATHER = (0, 1, 3, 4)
        COUNTED = (0, 3)
        rows_in = {p: [sem(f"rows_in{p}{j}") for j in range(IG)] for p in GATHER}
        idx_in = [sem(f"idx_in{h}") for h in range(2)]
        sel_ready = {p: sem(f"sel_ready{p}") for p in GATHER}
        aggs = {p: sem(f"aggs{p}") for p in GATHER}
        acc_done = {p: sem(f"acc_done{p}") for p in GATHER}
        moved = [sem(f"moved{p}") for p in range(5)]
        oh_ready, hist_mm, deg_ok, deg_zero = (sem(n) for n in ("oh_ready", "hist_mm", "deg_ok", "deg_zero"))
        emb_in = sem("emb_in")
        y_in = [sem(f"y_in{h}") for h in range(2)]
        h1_mm, h1_ok, h2_mm, h2_ok, w_mm = (sem(n) for n in ("h1_mm", "h1_ok", "h2_mm", "h2_ok", "w_mm"))
        s_wsel, s_t, s_scal, s_u = (sem(n) for n in ("s_wsel", "s_t", "s_scal", "s_u"))
        emb_pad = sem("emb_pad")
        s_dstl, s_srcl, s_rows16, s_rows_out, s_sidx, s_sidx_out = (
            sem(n) for n in ("s_dstl", "s_srcl", "s_rows16", "s_rows_out", "s_sidx", "s_sidx_out"))
        srow0_in = [sem(f"srow0_in{k}") for k in range(2)]
        same0_ok = sem("same0_ok")
        zero_out = sem("zero_out")
        pick_ok, same_ok, rows_mm, m_cp, comb_mm, scat_ok = (
            sem(n) for n in ("pick_ok", "same_ok", "rows_mm", "m_cp", "comb_mm", "scat_ok"))
        scat = [sem(f"scat{c}") for c in range(COPIES)]
        ring_free = sem("ring_free")
        srcc_in = [sem(f"srcc_in{h}") for h in range(2)]
        part_in = [sem(f"part_in{s}") for s in range(2)]
        msg_ok = [sem(f"msg_ok{p}") for p in range(2)]
        rbf_in = [sem(f"rbf_in{s}") for s in range(2)]
        c_mm, c_ok, m_mm = sem("c_mm"), sem("c_ok"), sem("m_mm")

        staged, projected, added, stats = (sem(n) for n in ("staged", "projected", "added", "stats"))
        s_var, s_sd, s_norm = sem("s_var"), sem("s_sd"), sem("s_norm")
        hrow_ok, turned, ht_ok, made, row_ok = (sem(n) for n in ("hrow_ok", "turned", "ht_ok", "made", "row_ok"))
        made0, row0_a, row0_v = sem("made0"), sem("row0_a"), sem("row0_v")
        normed, affine, keep_ok = sem("normed"), sem("affine"), sem("keep_ok")
        fin = sem("fin")
        row_out = [sem(f"row_out{s}") for s in range(2)]

        carried = sem("carried")
        credits = [(staged, 2), (projected, 2), (added, 2), (hrow_ok, 2), (turned, 2), (ht_ok, 2), (made, 2),
                   (row_ok, 2), (made0, 3), (row0_a, 2), (row0_v, 2), (hist_mm, 1), (deg_ok, 1),
                   (h1_mm, 1), (h1_ok, 1), (h2_mm, 1), (h2_ok, 1), (w_mm, 1), (c_mm, 4), (c_ok, 2), (m_mm, 2),
                   (same0_ok, 2), (rows_mm, 4), (same_ok, 3), (m_cp, 2), (comb_mm, 4), (scat_ok, 2), (ring_free, IG - 1)]
        credits += [(s, 1) for s in moved + row_out]
        credits += [(s, 4) for s in aggs.values()] + [(s, 2) for s in acc_done.values()] + [(s, 8) for s in msg_ok]

        block = ctx.enter_context(nc.Block())

        def rounds(eng):
            eng.wait_ge(s_nr, 1)
            return eng.value_load(NRI[0:1, 0:1], min_val=1, max_val=KV + 1)

        def apart(eng):
            eng.sem_inc(carried, 1)

        def stored(k):
            return 1 + (16 * (NB // 2 + UNITS * (k - 1)) if k else 0)

        def units_before(k, stages):
            return LASTU * sum(1 for j in stages if j < k)

        SUMS = (1, 2, 3, 4, 5)
        STAGED = (1, 2, 4, 5)
        HROWS = (0, 1, 2)
        ROWS = (1, 2, 3, 4, 5)

        @block.sync
        def _(sp):
            sp.dma_start(dst_i, dst).then_inc(s_dst, 16)
            sp.dma_start(work(EARLY_FROM, EARLY_N), early).then_inc(s_early, 16)
            for c in range(3):
                sp.dma_start(X[:, 25 * c:25 * c + 25, :], x[25 * c:25 * c + 25].rearrange("b p f -> p b f"))\
                  .then_inc(s_x[c], 16)
            sp.dma_start(src_i.rearrange("p (i t) -> p i t", t=IT), src.rearrange("i p t -> p i t")).then_inc(s_src, 16)
            sp.dma_start(typ_i, etype).then_inc(s_typ, 16)
            sp.dma_start(A1[:, 0:3 * TILES], evec).then_inc(s_vec, 16)
            sp.dma_start(dstl_i, dstl).then_inc(s_dstl, 16)
            sp.dma_start(srcl_i, srcl).then_inc(s_srcl, 16)
            sp.wait_ge(s_rows16, 2)
            sp.dma_start(drow_d.rearrange("(p g) n -> p (g n)", g=2), dstl_s).then_inc(s_rows_out, 16)
            sp.dma_start(srow_d.rearrange("(p g) n -> p (g n)", g=2), srcl_s).then_inc(s_rows_out, 16)
            sp.wait_ge(s_rows_out, 32)
            sp.dma_start(X[:, 75:100, :], x[75:100].rearrange("b p f -> p b f")).then_inc(s_x[3], 16)
            sp.wait_ge(s_idxc, 1)
            sp.dma_start(idx0.rearrange("i p t -> p i t"), idx_i.rearrange("p (i t) -> p i t", t=IT)).then_inc(s_idx0, 16)
            sp.wait_ge(s_idx0, 16)
            sp.wait_ge(s_nr, 1)
            sp.dma_start(A0[:, :], radii).then_inc(s_rad, 16)

            tab0_v = tab0.rearrange("(b p r) f -> b p (r f)", p=P, r=RELS)
            with sp.Fori(0, NB // 2) as i:
                for s in range(2):
                    sp.wait_ge(row0_a, 2 * i + s + 3)
                    sp.wait_ge(row0_v, 2 * i + s + 3)
                    sp.dma_start(tab0_v[ds(2 * i + s, 1)].rearrange("b p f -> (b p) f"), t0row[:, s])\
                      .then_inc(row_out[s], 16)

            nr = rounds(sp)
            sp.wait_ge(s_y, 1)
            sp.dma_start(y_d.rearrange("i p t -> p i t"), A1[:, 0:3 * TILES].rearrange("p (i t) -> p i t", t=3 * IT))\
              .then_inc(s_ystored, 16)
            sp.wait_ge(s_embok, 1)
            for h in range(2):
                sp.dma_start(emb_d[UNITS * h:UNITS * (h + 1)].rearrange("i q n -> q i n"),
                             A1[64 * h:64 * h + 64, :].rearrange("q (i n) -> q i n", n=512)).then_inc(s_emb, 16)
            sp.wait_ge(s_emb, 32)
            sp.dma_start(ew_t, eweight).then_inc(s_ewt, 16)
            sp.dma_start(srcs_i.rearrange("p (i t) -> p i t", t=IT), src.rearrange("i p t -> p i t")).then_inc(s_srcs, 16)

            def store_rows(k, table):
                view = table.rearrange("(b p) f -> b p f", p=P)
                with sp.Fori(0, UNITS) as i:
                    for s in range(2):
                        sp.wait_ge(row_ok, units_before(k, ROWS) + 2 * i + s + 3)
                        sp.dma_start(view[ds(4 * i + 2 * s, 2)].rearrange("b p f -> p b f"), trow[:, s])\
                          .then_inc(row_out[s], 16)

            def load_indices(p, h, i, n):
                if p == 1:
                    sp.wait_ge(msg_ok[0], 8 * n + 4 * h + 4)
                else:
                    sp.wait_ge(aggs[p], 4 * n + 2 * h + 2)
                apart(sp)
                sp.dma_start(IDX[:, h, :], (idx0 if p == 0 else src)[ds(i, 1), :, 16 * h:16 * h + 16]
                             .rearrange("a p t -> (a p) t")).then_inc(idx_in[h], 16)

            def index_pass(p):
                with sp.Fori(0, nr) as r:
                    with sp.Fori(0, ITS) as i:
                        n = r * ITS + i
                        for h in range(2):
                            load_indices(p, h, i, n)
                            for k in range(2 if p == 0 else 0):
                                g = 4 * n + 2 * h + k
                                sp.wait_ge(same0_ok, g + 1)
                                sp.dma_start(srow0[:, k], srow_d[ds(4 * i + 2 * h + k, 1), :].to_broadcast([P, GT * P]))\
                                  .then_inc(srow0_in[k], 16)

            index_pass(0)
            sp.wait_ge(s_sidx, 1)
            sp.dma_start(sidx.rearrange("i p t -> p i t"), sidx_i.rearrange("p (i t) -> p i t", t=IT)).then_inc(s_sidx_out, 16)
            store_rows(1, tabs[1])
            for s in range(2):
                sp.wait_ge(row_out[s], stored(2))
            with sp.Fori(0, nr) as r:
                with sp.Fori(0, ITS) as i:
                    n = r * ITS + i
                    load_indices(1, 0, i, n)
                    sp.wait_ge(h1_mm, 4 * n + 1)
                    sp.dma_start(emb[0:64, :], emb_d[ds(i, 1)].rearrange("a q n -> (a q) n")).then_inc(emb_in, 16)
                    for h in range(2):
                        if h == 1:
                            load_indices(1, 1, i, n)
                        sp.wait_ge(msg_ok[0], 8 * n + 4 * h + 4)
                        sp.dma_start(ybuf[:, h].rearrange("p t c -> p (t c)"),
                                     y_d[ds(i, 1), :, 48 * h:48 * h + 48].rearrange("a p t -> (a p) t"))\
                          .then_inc(y_in[h], 16)
            sp.wait_ge(s_zero0[2], 1)
            for acc in accs:
                sp.dma_start(acc.rearrange("(p b) f -> p (b f)", p=P), A0[:, :]).then_inc(zero_out, 16)
            store_rows(2, tabs[2])
            sp.wait_ge(zero_out, 16 * COPIES)
            for s in range(2):
                sp.wait_ge(row_out[s], stored(3))
            sp.dma_start(dsts_i, dst).then_inc(s_dsts, 16)
            with sp.Fori(0, nr) as r:
                sp.wait_ge(moved[2], 2 * r + 1)
                apart(sp)
                with sp.Fori(0, ITS) as i:
                    n = r * ITS + i
                    for j in range(IG):
                        g, h, k = 4 * n + j, j // 2, j % 2
                        if k == 0:
                            sp.wait_ge(same_ok, 4 * n + 2 * h + 1)
                            sp.dma_start(srcc[:, 16 * h:16 * h + 16], src[ds(i, 1), :, 16 * h:16 * h + 16]
                                         .rearrange("a p t -> (a p) t")).then_inc(srcc_in[h], 16)
                        start = sp.value_load(ADDR[0:1, ds(4 * i + j, 1)], min_val=0, max_val=ADDR_MAX)
                        sp.wait_ge(rows_mm, 2 * g + 2)
                        apart(sp)
                        sp.wait_ge(same_ok, g + 2)
                        sp.dma_start(rbf_t[:, k], rbf[ds(4 * i + j, 1)].rearrange("a p n -> (a p) n")).then_inc(rbf_in[k], 16)
                        sp.dma_start(srow[:, k], srow_d[ds(4 * i + j, 1), :].to_broadcast([P, GT * P])).then_inc(rbf_in[k], 16)
                        sp.dma_start(drow[0:W, k], drow_d[ds(4 * i + j, 1), :].to_broadcast([W, GT * P])).then_inc(rbf_in[k], 16)
                        sp.dma_start(twin[0:W, k], tabs[2][ds(start, W), :]).then_inc(rbf_in[k], 16)
                        if k == 1:
                            sp.wait_ge(ring_free, 4 * n + 2 * h + 2)
                            sp.dma_start(IDX[:, h, :], sidx[ds(i, 1), :, 16 * h:16 * h + 16]
                                         .rearrange("a p t -> (a p) t")).then_inc(idx_in[h], 16)
            for c in range(COPIES):
                sp.wait_ge(scat[c], 16 * 2 * GROUPS * nr)
                apart(sp)
            with sp.Fori(0, UNITS) as i:
                for s in range(2):
                    sp.wait_ge(projected, units_before(3, SUMS) + 2 * i + s + 1)
                    for c, acc in enumerate(accs):
                        sp.dma_start(parts[:, s, c, :].rearrange("p (b f) -> p b f", b=2),
                                     acc.rearrange("(b p) f -> b p f", p=P)[ds(4 * i + 2 * s, 2)]
                                     .rearrange("b p f -> p b f")).then_inc(part_in[s], 16)
            store_rows(3, tabs[3])
            index_pass(3)
            store_rows(4, tabs[4])
            index_pass(4)
            store_rows(5, out)
            for s in range(2):
                sp.wait_ge(row_out[s], stored(6))

        @block.gpsimd
        def _(pool):
            pool.wait_ge(s_gmin, 1)
            pool.partition_all_reduce(base, gmin, P, MAX).then_inc(s_gall, 1)
            pool.wait_ge(s_dmax, 1)
            pool.partition_all_reduce(dmax[:, 1:2], dmax[:, 0:1], P, MAX).then_inc(s_dall, 1)
            nr = rounds(pool)
            pool.wait_ge(s_embok, 1)
            pool.memset(A0[:, :], 0.0).then_inc(s_zero0[0], 1)

            def scatter_pass():
                def turn2(n, is_first):
                    for j in range(IG):
                        if j % 2 == 0:
                            pool.wait_ge(idx_in[j // 2], 16 * (2 * ITS * nr + n + 1))
                        for t in range(GT):
                            if t % 4 == 0:
                                pool.wait_ge(scat_ok, 2 * (4 * n + j) + t // 4 + 3)
                            c = t % COPIES
                            if not (is_first and j == 0 and t < COPIES):
                                pool.wait_ge(scat[c], 16 * (2 * (4 * n + j) + t // COPIES))
                            if t == COPIES - 1:
                                pool.sem_inc(ring_free, 1)
                            else:
                                apart(pool)
                            col = GT * (j % 2) + t
                            pool.indirect_dma_start(accs[c], bass.IndirectOffsetOnAxis(IDX[:, j // 2, col:col + 1], 0),
                                                    ring[:, j, t, :], None, compute_op=ALU.add).then_inc(scat[c], 16)

                with pool.Fori(0, nr) as r:
                    turn2(r * ITS, True)
                    with pool.Fori(0, ITS - 1) as i:
                        turn2(r * ITS + i + 1, False)
                    for c in range(COPIES):
                        pool.wait_ge(scat[c], 16 * 2 * GROUPS * (r + 1))

            for p in range(5):
                for s in range(2):
                    pool.wait_ge(row_out[s], stored(p + 1))
                if p == 2:
                    pool.wait_ge(zero_out, 16 * COPIES)
                    pool.wait_ge(s_sidx_out, 16)
                    scatter_pass()
                    pool.wait_ge(projected, 2 + units_before(4, SUMS))
                    pool.memset(A0[:, :], 0.0).then_inc(s_zero0[3], 1)
                    continue
                with pool.Fori(0, nr) as r:
                    with pool.Fori(0, ITS) as i:
                        n = r * ITS + i
                        for j in range(IG):
                            if j % 2 == 0:
                                pool.wait_ge(idx_in[j // 2], 16 * (p * ITS * nr + n + 1))
                            if p == 1:
                                pool.wait_ge(msg_ok[0], 2 * (4 * n + j) + 2)
                            else:
                                pool.wait_ge(aggs[p], 4 * n + j + 1)
                            apart(pool)
                            for t in range(GT):
                                c = GT * (j % 2) + t
                                pool.indirect_dma_start(ring[:, j, t, :], None, tabs[p],
                                                        bass.IndirectOffsetOnAxis(IDX[:, j // 2, c:c + 1], 0))\
                                    .then_inc(rows_in[p][j], 16)
                if p == 0:
                    pool.wait_ge(acc_done[0], 2 + GROUPS * nr)
                    apart(pool)
                    pool.wait_ge(s_sidx_out, 16)
                    pool.memset(A1[:, :], 0.0).then_inc(s_zero1, 1)
                if p < 4:
                    pool.wait_ge(staged, 2 + units_before(p + 2, STAGED))
                    pool.memset(A0[:, :], 0.0).then_inc(s_zero0[p + 1], 1)

        @block.scalar
        def _(act):
            act.dma_start(R[:, :], resident).then_inc(s_res, 16)
            act.wait_ge(s_res, 16)

            def root(which):
                act.wait_ge(s_var, which + 1)
                nc.scalar.activation(rstd, var, ACT.Sqrt, bias=res("eps")).then_inc(s_sd, 1)

            def degree_roots(k):
                act.wait_ge(s_deg, k + 1)
                nc.scalar.activation(DEG[:, k], DEG[:, k], ACT.Sqrt).then_inc(s_degr, 1)

            def stage_sums(k):
                halves = (A0, A1) if k == 2 else (A0,)
                with act.Fori(0, UNITS) as i:
                    for s in range(2):
                        u = units_before(k, SUMS) + 2 * i + s
                        act.wait_ge(projected, u + 1)
                        for a, half in enumerate(halves):
                            last = nc.scalar.activation(stage[:, s, a, :], half[:, ds(256 * (2 * i + s), 256)], ACT.Copy)
                        last.then_inc(staged, 1)

            root(0)
            act.wait_ge(s_norm, 1)
            with act.Fori(0, UNITS) as i:
                for s in range(2):
                    u = 2 * i + s
                    act.wait_ge(turned, u + 1)
                    for b in range(2):
                        at = ds(2 * u + b, 1)
                        last = nc.scalar.activation(hrow[:, s, b, :], X[:, at, :].rearrange("p b f -> p (b f)"), ACT.Relu,
                                                    bias=nmr[:, at], scale=rstd[:, at])
                    last.then_inc(hrow_ok, 1)
                    for b in range(2):
                        act.wait_ge(made0, 2 * u + b + 4)
                        act.wait_ge(row_out[b], stored(0) + 16 * u)
                        nc.scalar.activation(t0row[:, b, 0:512], BANK[4 + 2 * b][:, :], ACT.Copy).then_inc(row0_a, 1)

            nr = rounds(act)
            act.wait_ge(s_ysum, 1)
            nc.scalar.activation(vlen, vlen, ACT.Sqrt).then_inc(s_ysq, 1)
            act.wait_ge(s_clip, 1)
            nc.scalar.activation(A1[:, :], A1[:, :], ACT.Square, bias=res("ncen"), scale=float(CENTERS - 1)).then_inc(s_sq, 1)
            act.wait_ge(s_sq, 1)
            nc.scalar.activation(A1[:, :], A1[:, :], ACT.Exp, scale=-0.5).then_inc(s_exp, 1)

            act.wait_ge(acc_done[0], 2 + GROUPS * nr)
            stage_sums(1)
            degree_roots(0)
            root(1)

            def transposed_rows(k, which):
                act.wait_ge(s_norm, which + 1)
                with act.Fori(0, UNITS) as i:
                    for s in range(2):
                        u = units_before(k, HROWS) + 2 * i + s
                        act.wait_ge(turned, u + 1)
                        for b in range(2):
                            at = ds(2 * (2 * i + s) + b, 1)
                            last = nc.scalar.activation(hrow[:, s, b, :], X[:, at, :].rearrange("p b f -> p (b f)"),
                                                        ACT.Relu, bias=nmr[:, at], scale=rstd[:, at])
                        last.then_inc(hrow_ok, 1)
                        if k == 2:
                            act.wait_ge(hrow_ok, u + 3)
                            nc.scalar.activation(A1[:, ds(256 * (2 * i + s), 256)],
                                                 hrow[:, s].rearrange("p b f -> p (b f)"), ACT.Copy).then_inc(keep_ok, 1)

            transposed_rows(1, 1)

            with act.Fori(0, nr) as r:
                with act.Fori(0, ITS) as i:
                    for j in range(IG):
                        g = 4 * (r * ITS + i) + j
                        act.wait_ge(h1_mm, g + 2)
                        act.wait_ge(h2_mm, g + 1)
                        nc.scalar.activation(h1, BANK[0][:, :], ACT.Silu, bias=res("mb0")).then_inc(h1_ok, 1)
                        act.wait_ge(h2_mm, g + 2)
                        act.wait_ge(w_mm, 2 * g + 1)
                        nc.scalar.activation(h2, BANK[1][:, :], ACT.Silu, bias=res("mb1")).then_inc(h2_ok, 1)

            act.wait_ge(acc_done[1], 2 + GROUPS * nr)
            stage_sums(2)
            root(2)
            transposed_rows(2, 2)

            def silu2(m, s):
                act.wait_ge(c_mm, m + 5)
                act.wait_ge(m_mm, m + 1)
                nc.scalar.activation(hs2[:, s], BANK[s][:, :], ACT.Silu, bias=res("cb0")).then_inc(c_ok, 1)

            def copy_m(m, s):
                act.wait_ge(m_mm, m + 3)
                act.wait_ge(msg_ok[1], m + 7)
                nc.scalar.activation(mout[:, s], BANK[2 + s][:, :], ACT.Copy).then_inc(m_cp, 1)

            def copy_sums(n, j, m, s):
                act.wait_ge(comb_mm, m + 5)
                if s == 0:
                    act.wait_ge(ring_free, 4 * n + j + 1)
                nc.scalar.activation(ring[:, j, 4 * s:4 * s + 4, :].rearrange("p t f -> p (t f)"), BANK[6 + s][:, :],
                                     ACT.Copy).then_inc(scat_ok, 1)

            act.wait_ge(zero_out, 16 * COPIES)
            for s in range(2):
                act.wait_ge(row_out[s], stored(3))
            with act.Fori(0, nr) as r:
                def turn2(n, is_last):
                    for q in range(2 * IG):
                        if q + 1 < 2 * IG or not is_last:
                            silu2(8 * n + q + 1, (q + 1) % 2)
                        copy_m(8 * n + q, q % 2)
                        if q:
                            copy_sums(n, (q - 1) // 2, 8 * n + q - 1, (q - 1) % 2)
                    copy_sums(n, IG - 1, 8 * n + 2 * IG - 1, 1)

                n0 = r * ITS
                silu2(8 * n0, 0)
                with act.Fori(0, ITS - 1) as i:
                    turn2(n0 + i, False)
                turn2(n0 + ITS - 1, True)

            root(3)
            act.wait_ge(s_norm, 4)
            with act.Fori(0, UNITS) as i:
                for s in range(2):
                    for b in range(2):
                        c = 2 * (2 * i + s) + b
                        h = A1[:, ds(128 * c, 128)]
                        last = nc.scalar.activation(h, h, ACT.Identity, bias=nmr[:, ds(c, 1)], scale=rstd[:, ds(c, 1)])
                    last.then_inc(normed, 1)
            root(4)
            act.wait_ge(s_norm, 5)
            with act.Fori(0, UNITS) as i:
                for s in range(2):
                    for b in range(2):
                        c = 2 * (2 * i + s) + b
                        last = nc.scalar.activation(A1[:, ds(128 * c, 128)], X[:, ds(c, 1), :].rearrange("p b f -> p (b f)"),
                                                    ACT.Relu, bias=nmr[:, ds(c, 1)], scale=rstd[:, ds(c, 1)])
                    last.then_inc(normed, 1)
            for p in (3, 4):
                act.wait_ge(acc_done[p], 2 + GROUPS * nr)
                if p == 3:
                    degree_roots(1)
                stage_sums(p + 1)

        @block.vector
        def _(v):
            done = [0]

            def step(ins):
                done[0] += 1
                ins.then_inc(chain, 1)
                v.wait_ge(chain, done[0])

            for s, n in credits:
                v.sem_inc(s, n)

            v.wait_ge(s_dst, 16)
            step(v.tensor_copy(DREL[:, :], dst_i))
            v.tensor_reduce(gmin, DREL[:, :].rearrange("p (g t) -> p g t", t=GT), AX.X, ALU.min, negate=True)\
             .then_inc(s_gmin, 1)
            v.wait_ge(s_gall, 1)
            step(v.tensor_scalar(base, base, -1.0, None, ALU.mult))
            drel_g = DREL[:, :].rearrange("p (g t) -> p g t", t=GT)
            step(v.tensor_tensor(drel_g, drel_g, base.unsqueeze(2).to_broadcast([P, GROUPS, GT]), ALU.subtract))
            step(v.tensor_copy(ADDR0[:, :], base[0:1, :]))
            step(v.tensor_copy(ADDR[:, :], ADDR0[:, :]))
            v.tensor_reduce(dmax[:, 0:1], DREL[:, :], AX.X, ALU.max).then_inc(s_dmax, 1)
            v.wait_ge(s_dall, 1)
            v.wait_ge(s_early, 16)
            step(v.tensor_scalar(kcmp, early_w("kvec"), dmax[:, 1:2], None, ALU.is_le))
            step(v.tensor_reduce(NRW[:, :], kcmp, AX.X, ALU.add))
            step(v.tensor_scalar(NRW[:, :], NRW[:, :], 1.0, None, ALU.add))
            step(v.tensor_copy(NRI[:, :], NRW[0:1, :]))
            v.tensor_scalar(NRW[:, :], NRW[:, :], float(W), None, ALU.mult).then_inc(s_nr, 1)

            v.wait_ge(s_dstl, 16)
            lin = dstl_i.rearrange("p (g n) -> p g n", g=2)
            step(v.tensor_reduce(low, lin, AX.X, ALU.min))
            v.tensor_tensor(dstl_s.rearrange("p (g n) -> p g n", g=2), lin,
                            low.unsqueeze(2).to_broadcast([LIN, 2, GT * P]), ALU.subtract).then_inc(s_rows16, 1)
            v.wait_ge(s_srcl, 16)
            v.tensor_copy(srcl_s, srcl_i).then_inc(s_rows16, 1)

            v.wait_ge(s_src, 16)
            v.wait_ge(s_typ, 16)
            v.scalar_tensor_tensor(out=idx_i, in0=src_i, scalar=float(RELS), in1=typ_i, op0=ALU.mult, op1=ALU.add)\
             .then_inc(s_idxc, 1)
            v.wait_ge(s_nr, 1)
            nr = rounds(v)

            bases = early_w("bases").rearrange("p (b f) -> p b f", b=BASES)
            for rel in range(RELS):
                m = wall[:, 128 * rel:128 * rel + 128]
                for b in range(BASES):
                    k = rel * BASES + b
                    coef = early_w("wcomp")[:, k:k + 1]
                    if b == 0:
                        step(v.tensor_scalar(m, bases[:, b], coef, None, ALU.mult))
                    else:
                        step(v.scalar_tensor_tensor(out=m, in0=bases[:, b], scalar=coef, in1=m, op0=ALU.mult, op1=ALU.add))
            v.wait_ge(s_res, 16)
            step(v.tensor_copy(IOB[:, :], early_w("iota")))
            step(v.tensor_copy(NODE[:, :], res("rowno")))
            step(v.memset(ONES[:, :], 1.0))
            for k, name in enumerate(("b2a", "b2b")):
                rest = early_w(name)
                step(v.tensor_scalar(b2f, rest, res("rowm")[:, 0:1], None, ALU.mult))
                for part in (1, 2):
                    step(v.tensor_copy(B2S[:, k, :], rest))
                    step(v.tensor_tensor(rest, rest, B2S[:, k, :], ALU.subtract))
                    step(v.scalar_tensor_tensor(out=b2f, in0=rest, scalar=res("rowm")[:, part:part + 1], in1=b2f,
                                                op0=ALU.mult, op1=ALU.add))
                step(v.tensor_copy(B2S[:, k, :], b2f))
            step(v.tensor_scalar(res("ew"), res("ew"), float(CENTERS) ** 0.5, None, ALU.mult))
            v.tensor_scalar(res("woa")[32:64, :], res("woa")[32:64, :], 3.0 ** -0.5, None, ALU.mult).then_inc(s_ew, 1)
            v.wait_ge(s_cmm, 1)
            v.tensor_copy(CW[:, :], BANK[7][:, 0:128]).then_inc(s_cok, 1)

            def finish_stats(which):
                v.wait_ge(stats, LASTU * (which + 1))
                step(v.tensor_tensor(mean, stat[:, :, 1], stat[:, :, 4], ALU.add))
                step(v.tensor_tensor(dif, stat[:, :, 1], stat[:, :, 4], ALU.subtract))
                step(v.tensor_tensor(var, stat[:, :, 2], stat[:, :, 5], ALU.add))
                step(v.tensor_tensor(dif, dif, dif, ALU.mult))
                step(v.tensor_scalar(dif, dif, 0.25, None, ALU.mult))
                v.scalar_tensor_tensor(out=var, in0=var, scalar=1.0 / FEAT, in1=dif, op0=ALU.mult, op1=ALU.add)\
                 .then_inc(s_var, 1)
                v.wait_ge(s_sd, which + 1)
                step(v.reciprocal(rstd, rstd))
                v.scalar_tensor_tensor(out=nmr, in0=mean, scalar=-0.5, in1=rstd, op0=ALU.mult, op1=ALU.mult)\
                 .then_inc(s_norm, 1)

            def row_stats(rows_of, b0):
                for b in range(2):
                    at = ds(b0 + b, 1)
                    last = v.bn_stats(stat[:, at, :].rearrange("p b c -> p (b c)"), rows_of(b))
                last.then_inc(stats, 1)

            def x_block(c):
                return X[:, ds(c, 1), :].rearrange("p b f -> p (b f)")

            for c in range(4):
                v.wait_ge(s_x[c], 16)
            with v.Fori(0, UNITS) as i:
                for s in range(2):
                    c = 2 * (2 * i + s)
                    row_stats(lambda b: x_block(c + b), c)
            finish_stats(0)
            with v.Fori(0, UNITS) as i:
                for s in range(2):
                    u = 2 * i + s
                    v.wait_ge(turned, u + 3)
                    v.wait_ge(made0, 2 * u + 1)
                    v.tensor_copy(hT[:, s].rearrange("p b f -> p (b f)"), BANK[2 + s][:, 0:256]).then_inc(ht_ok, 1)
                    for b in range(2):
                        v.wait_ge(made0, 2 * u + b + 4)
                        v.wait_ge(row_out[b], stored(0) + 16 * u)
                        v.tensor_copy(t0row[:, b, 512:1024], BANK[5 + 2 * b][:, :]).then_inc(row0_v, 1)

            v.wait_ge(s_vec, 16)
            step(v.tensor_tensor(vsq, vec, vec, ALU.mult))
            step(v.tensor_reduce(vlen, vsq, AX.X, ALU.add))
            v.tensor_scalar(vlen, vlen, 1.3e-35, None, ALU.max).then_inc(s_ysum, 1)
            v.wait_ge(s_ysq, 1)
            step(v.tensor_scalar(vlen, vlen, 1e-12, None, ALU.add))
            step(v.reciprocal(vlen, vlen))
            step(v.tensor_scalar(vlen, vlen, 3.0 ** 0.5, None, ALU.mult))
            v.tensor_tensor(vec, vec, vlen.unsqueeze(2).to_broadcast([P, TILES, 3]), ALU.mult).then_inc(s_y, 1)
            v.wait_ge(s_rad, 16)
            v.wait_ge(s_ystored, 16)
            v.tensor_scalar(A1[:, :], A0[:, :], 0.0, 1.0, ALU.max, ALU.min).then_inc(s_clip, 1)
            v.wait_ge(s_exp, 1)
            v.scalar_tensor_tensor(out=A1[:, :], in0=A0[:, :], scalar=1.0, in1=A1[:, :], op0=ALU.is_le, op1=ALU.mult)\
             .then_inc(s_embok, 1)

            def split_bits(ints, part, bits):
                step(v.tensor_scalar(part, ints, P - 1, None, ALU.bitwise_and))
                step(v.tensor_copy(bits[:, 0], part))
                step(v.tensor_scalar(part, ints, 7, None, ALU.logical_shift_right))
                step(v.tensor_copy(bits[:, 1], part))

            v.wait_ge(s_srcs, 16)
            split_bits(srcs_i, part_i, src_bits)
            step(v.tensor_copy(beforeb, early_w("before")))
            v.wait_ge(s_ewt, 16)

            def group_tiles(array, i, j):
                return array[:, ds(GT * (4 * i + j), GT)]

            def select(p, i, j, g):
                if p == 1:
                    v.wait_ge(aggs[p], 2 * g + 2)
                else:
                    v.wait_ge(aggs[p], g + 3)
                at = sel[:, j % 2]
                eq = v.tensor_tensor(at, IOB[:, 0:W].unsqueeze(1).to_broadcast([P, GT, W]),
                                     group_tiles(DREL, i, j).unsqueeze(2).to_broadcast([P, GT, W]), ALU.is_equal)
                if p == 0:
                    eq.then_inc(s_wsel, 1)
                    v.wait_ge(s_wsel, g + 1)
                    eq = v.tensor_tensor(at, at, group_tiles(ew_t, i, j).unsqueeze(2).to_broadcast([P, GT, W]), ALU.mult)
                eq.then_inc(sel_ready[p], 1)

            def accumulate(p, i, j, g):
                start = v.value_load(ADDR[0:1, ds(4 * i + j, 1)], min_val=0, max_val=ADDR_MAX)
                v.wait_ge(aggs[p], 2 * g + 6 if p == 1 else g + 5)
                v.wait_ge(acc_done[p], g + 2)
                if p == 1:
                    part = A1[:, ds(start, W)]
                    v.tensor_tensor(part, part, BANK[6 + j % 2][:, 0:W], ALU.add)
                part = A0[:, ds(start, W)]
                v.tensor_tensor(part, part, BANK[4 + j % 2][:, 0:W], ALU.add).then_inc(acc_done[p], 1)

            def move_windows(p, r):
                v.wait_ge(sel_ready[p], GROUPS * (r + 1))
                v.tensor_scalar(DREL[:, :], DREL[:, :], float(W), None, ALU.subtract).then_inc(moved[p], 1)
                v.tensor_scalar(ADDR[:, :], ADDR[:, :], float(W), float(ADDR_MAX), ALU.add, ALU.min).then_inc(moved[p], 1)

            def reset_windows(p):
                v.wait_ge(moved[p], 2 * nr + 1)
                step(v.tensor_scalar(DREL[:, :], DREL[:, :], NRW[:, 0:1], None, ALU.add))
                step(v.tensor_copy(ADDR[:, :], ADDR0[:, :]))

            def plain_pass(p):
                deg = DEG[:, COUNTED.index(p)] if p in COUNTED else None
                v.wait_ge(s_zero0[p], 1)
                with v.Fori(0, nr) as r:
                    v.wait_ge(moved[p], 2 * r + 1)
                    apart(v)
                    if p in COUNTED:
                        before = COUNTED.index(p) * nr
                        v.wait_ge(deg_ok, GROUPS * (before + r) + 1)
                        apart(v)
                        v.memset(deg, 0.0).then_inc(deg_zero, 1)
                        v.wait_ge(deg_zero, before + r + 1)
                        apart(v)
                    with v.Fori(0, ITS) as i:
                        n = r * ITS + i
                        for j in range(IG):
                            g = 4 * n + j
                            if p in COUNTED:
                                bits = src_bits if p == 0 else dst_bits
                                c = COUNTED.index(p) * GROUPS * nr + g
                                v.wait_ge(hist_mm, c + 1)
                                for k, (at, wide) in enumerate(((0, P), (P, NB))):
                                    last = v.tensor_tensor(oh[:, :, at:at + wide],
                                                           IOB[:, 0:wide].unsqueeze(1).to_broadcast([P, GT, wide]),
                                                           group_tiles(bits[:, k], i, j).unsqueeze(2)
                                                           .to_broadcast([P, GT, wide]), ALU.is_equal)
                                last.then_inc(oh_ready, 1)
                            if p == 0:
                                v.wait_ge(srow0_in[j % 2], 16 * (2 * n + j // 2 + 1))
                                for t in range(GT):
                                    tile = GT * (4 * i + j) + t
                                    last = v.scalar_tensor_tensor(
                                        out=same0[:, t, :], in0=srow0[:, j % 2, P * t:P * t + P],
                                        scalar=srcs_i[:, ds(tile, 1)], in1=beforeb,
                                        op0=ALU.is_equal, op1=ALU.mult, accum_out=earlier[:, ds(tile, 1)])
                                last.then_inc(same0_ok, 1)
                            select(p, i, j, g)
                            if p in COUNTED:
                                v.wait_ge(hist_mm, c + 2)
                                v.wait_ge(deg_ok, c + 1)
                                v.tensor_tensor(deg, deg, BANK[6][:, 0:NB], ALU.add).then_inc(deg_ok, 1)
                            if j:
                                accumulate(p, i, j - 1, g - 1)
                        accumulate(p, i, IG - 1, 4 * n + IG - 1)
                    move_windows(p, r)
                reset_windows(p)

            def sums(k, add):
                with v.Fori(0, UNITS) as i:
                    for s in range(2):
                        u = 2 * i + s
                        v.wait_ge(projected, units_before(k, SUMS) + u + 3)
                        add(u, s)

            def add_to(k, rows, scale):
                def add(u, s):
                    both = rows[:, ds(2 * u, 2), :]
                    v.scalar_tensor_tensor(out=both, in0=BANK[s][:, 0:256].rearrange("p (b f) -> p b f", b=2), scalar=scale,
                                           in1=both, op0=ALU.mult, op1=ALU.add).then_inc(added, 1)
                    v.wait_ge(added, units_before(k, SUMS) + u + 3)
                    row_stats(lambda b: rows[:, ds(2 * u + b, 1), :].rearrange("p b f -> p (b f)"), 2 * u)
                return add

            plain_pass(0)

            def clip_degrees(k):
                v.wait_ge(deg_ok, (k + 1) * (GROUPS * nr) + 1)
                v.tensor_scalar(DEG[:, k], DEG[:, k], 1.0, None, ALU.max).then_inc(s_deg, 1)

            def invert_roots(k):
                v.wait_ge(s_degr, k + 1)
                step(v.reciprocal(DEG[:, k], DEG[:, k]))

            v.wait_ge(same0_ok, GROUPS * nr + 2)
            step(v.tensor_scalar(sidx_f, res("rowno").to_broadcast([P, TILES]), float(SPARE), None, ALU.add))
            step(v.tensor_tensor(sidx_f, sidx_f, srcs_i, ALU.subtract))
            step(v.scalar_tensor_tensor(out=sidx_f, in0=earlier, scalar=1.0, in1=sidx_f, op0=ALU.min, op1=ALU.mult))
            v.tensor_tensor(sidx_i, sidx_f, srcs_i, ALU.add).then_inc(s_sidx, 1)

            clip_degrees(0)
            sums(1, add_to(1, X, 1.0))
            invert_roots(0)
            finish_stats(1)
            A1r = A1[:, :].rearrange("p (b f) -> p b f", f=FEAT)

            def table_rows(k):
                with v.Fori(0, UNITS) as i:
                    for s in range(2):
                        u = units_before(k, HROWS) + 2 * i + s
                        w = units_before(k, (1, 2)) + 2 * i + s
                        v.wait_ge(turned, u + 3)
                        v.wait_ge(made, w + 1)
                        v.tensor_copy(hT[:, s].rearrange("p b f -> p (b f)"), BANK[2 + s][:, 0:256]).then_inc(ht_ok, 1)
                        v.wait_ge(made, w + 3)
                        v.wait_ge(row_out[s], stored(k) + 16 * i)
                        made_v = BANK[4 + s][:, 0:256].rearrange("p (b f) -> p b f", b=2)
                        if k == 1:
                            ins = v.tensor_scalar(trow[:, s], made_v, float(MUL) ** -0.5, None, ALU.mult)
                        else:
                            ins = v.tensor_tensor(trow[:, s], made_v, res("bl").unsqueeze(1).to_broadcast([P, 2, FEAT]), ALU.add)
                        ins.then_inc(row_ok, 1)

            table_rows(1)

            def messages1(i, j, s, m):
                h, t0 = j // 2, GT * (j % 2) + 4 * s
                w4 = BANK[2 + s][:, :].rearrange("p (t k m) -> p t k m", t=4, k=4)
                rows = ring[:, j, 4 * s:4 * s + 4, :]
                sc = rows[:, :, 0:32]
                scal, ubuf = scals[:, s], ubufs[:, s]
                vv = rows[:, :, 32:128].rearrange("p t (c m) -> p t c m", c=3)
                M = msg1[:, s]
                m1 = M[:, :, 64:160].rearrange("p t (c m) -> p t c m", c=3)
                m2 = M[:, :, 160:256].rearrange("p t (c m) -> p t c m", c=3)
                y = ybuf[:, h, t0:t0 + 4, :].unsqueeze(3).to_broadcast([P, 4, 3, 32])
                v.wait_ge(aggs[1], m + 3)
                v.tensor_tensor(m2, vv, y, ALU.mult).then_inc(s_t, 1)
                v.wait_ge(w_mm, m + 2)
                v.tensor_tensor(scal, w4[:, :, 1], sc, ALU.mult).then_inc(s_scal, 1)
                v.wait_ge(s_t, m + 1)
                v.tensor_tensor(ubuf, m2[:, :, 0], m2[:, :, 1], ALU.add).then_inc(s_u, 1)
                v.tensor_tensor(M[:, :, 0:32], w4[:, :, 0], sc, ALU.mult)
                v.wait_ge(s_u, 2 * m + 1)
                v.tensor_tensor(ubuf, ubuf, m2[:, :, 2], ALU.add).then_inc(s_u, 1)
                v.wait_ge(s_scal, m + 1)
                v.tensor_tensor(m1, scal.unsqueeze(2).to_broadcast([P, 4, 3, 32]), y, ALU.mult)
                v.wait_ge(s_u, 2 * m + 2)
                v.tensor_tensor(M[:, :, 32:64], w4[:, :, 3], ubuf, ALU.mult)
                v.tensor_tensor(m2, vv, w4[:, :, 2].unsqueeze(2).to_broadcast([P, 4, 3, 32]), ALU.mult).then_inc(msg_ok[0], 1)

            for s in range(2):
                v.wait_ge(row_out[s], stored(2))
            v.memset(emb[64:128, :], 0.0).then_inc(emb_pad, 1)
            v.wait_ge(s_zero0[1], 1)
            v.wait_ge(s_zero1, 1)
            with v.Fori(0, nr) as r:
                v.wait_ge(moved[1], 2 * r + 1)
                apart(v)
                with v.Fori(0, ITS) as i:
                    n = r * ITS + i
                    for j in range(IG):
                        g = 4 * n + j
                        if j % 2 == 0:
                            v.wait_ge(y_in[j // 2], 16 * (n + 1))
                        select(1, i, j, g)
                        v.wait_ge(rows_in[1][j], 16 * GT * (n + 1))
                        messages1(i, j, 0, 2 * g)
                        if j:
                            accumulate(1, i, j - 1, g - 1)
                        messages1(i, j, 1, 2 * g + 1)
                    accumulate(1, i, IG - 1, 4 * n + IG - 1)
                move_windows(1, r)
            reset_windows(1)

            sums(2, add_to(2, X, 1.0 / (8.0 * 16.0)))
            finish_stats(2)
            table_rows(2)

            v.wait_ge(s_dsts, 16)
            split_bits(dsts_i, dpart_i, dst_bits)
            v.wait_ge(zero_out, 16 * COPIES)

            def pick_rows(n, j):
                g = 4 * n + j
                v.wait_ge(rbf_in[j % 2], 64 * (2 * n + j // 2 + 1))
                v.wait_ge(rows_mm, 2 * g + 2)
                v.tensor_scalar(pick[0:W, j % 2], drow[0:W, j % 2], NODE[0:W, 0:1], None, ALU.is_equal).then_inc(pick_ok, 1)

            def same_source(n, j):
                g = 4 * n + j
                if j % 2 == 0:
                    v.wait_ge(srcc_in[j // 2], 16 * (n + 1))
                v.wait_ge(comb_mm, 2 * g + 2)
                for t in range(GT):
                    c = GT * j + t
                    last = v.tensor_scalar(same[:, j % 2, t, :], srow[:, j % 2, P * t:P * t + P], srcc[:, c:c + 1], None,
                                           ALU.is_equal)
                last.then_inc(same_ok, 1)

            with v.Fori(0, nr) as r:
                v.wait_ge(moved[2], 2 * r + 1)
                apart(v)
                def turn2(n, is_last):
                    for j in range(IG):
                        after = (n, j + 1) if j + 1 < IG else (n + 1, 0)
                        more = j + 1 < IG or not is_last
                        for s in range(2):
                            if s == 1 and more:
                                pick_rows(*after)
                            m = 2 * (4 * n + j) + s
                            v.wait_ge(m_cp, m + 3)
                            v.wait_ge(rows_mm, m + 5)
                            v.wait_ge(comb_mm, m + 3)
                            v.tensor_tensor(msg2[:, s].rearrange("p t f -> p (t f)"), mout[:, s], BANK[4 + s][:, :],
                                            ALU.mult).then_inc(msg_ok[1], 1)
                            if s == 1 and more:
                                same_source(*after)

                n0 = r * ITS
                pick_rows(n0, 0)
                same_source(n0, 0)
                with v.Fori(0, ITS - 1) as i:
                    turn2(n0 + i, False)
                turn2(n0 + ITS - 1, True)
                v.wait_ge(pick_ok, GROUPS * (r + 1))
                v.tensor_scalar(NODE[:, :], NODE[:, :], float(W), None, ALU.add).then_inc(moved[2], 1)
                v.tensor_scalar(ADDR[:, :], ADDR[:, :], float(W), float(ADDR_MAX), ALU.add, ALU.min).then_inc(moved[2], 1)
            v.wait_ge(moved[2], 2 * nr + 1)
            step(v.tensor_copy(ADDR[:, :], ADDR0[:, :]))

            v.wait_ge(keep_ok, LASTU)
            sums(3, add_to(3, A1r, 1.0))
            finish_stats(3)
            with v.Fori(0, UNITS) as i:
                for s in range(2):
                    u = 2 * i + s
                    tmp = hT[:, s]
                    v.wait_ge(normed, u + 1)
                    v.tensor_tensor(tmp, A1r[:, ds(2 * u, 2), :], res("gamma").unsqueeze(1).to_broadcast([P, 2, FEAT]),
                                    ALU.mult).then_inc(affine, 1)
                    v.wait_ge(affine, 3 * u + 1)
                    v.tensor_tensor(tmp, tmp, res("beta").unsqueeze(1).to_broadcast([P, 2, FEAT]), ALU.add).then_inc(affine, 1)
                    v.wait_ge(affine, 3 * u + 2)
                    v.tensor_tensor(X[:, ds(2 * u, 2), :], X[:, ds(2 * u, 2), :], tmp, ALU.add).then_inc(affine, 1)
                    v.wait_ge(affine, 3 * u + 3)
                    row_stats(lambda b: x_block(2 * u + b), 2 * u)
            finish_stats(4)
            with v.Fori(0, UNITS) as i:
                for s in range(2):
                    u = 2 * i + s
                    v.wait_ge(normed, LASTU + u + 1)
                    v.wait_ge(row_out[s], stored(3) + 16 * i)
                    v.tensor_tensor(trow[:, s], A1r[:, ds(2 * u, 2), :],
                                    DEG[:, 0, ds(2 * u, 2)].unsqueeze(2).to_broadcast([P, 2, FEAT]), ALU.mult)\
                     .then_inc(row_ok, 1)

            def conv_rows(k, bias):
                def add(u, s):
                    t, rows = hT[:, s], trow[:, s]
                    n0 = 2 * u if k == 4 else 2 * LASTU + 3 * u
                    v.tensor_tensor(t, BANK[s][:, 0:256].rearrange("p (b f) -> p b f", b=2),
                                    DEG[:, 1, ds(2 * u, 2)].unsqueeze(2).to_broadcast([P, 2, FEAT]), ALU.mult)\
                     .then_inc(added, 1)
                    v.wait_ge(added, units_before(k, SUMS) + u + 3)
                    v.tensor_tensor(t, t, res(bias).unsqueeze(1).to_broadcast([P, 2, FEAT]), ALU.add).then_inc(fin, 1)
                    v.wait_ge(fin, n0 + 1)
                    v.scalar_tensor_tensor(out=t, in0=t, scalar=0.0, in1=A1r[:, ds(2 * u, 2), :], op0=ALU.max, op1=ALU.add)\
                     .then_inc(fin, 1)
                    v.wait_ge(fin, n0 + 2)
                    if k == 5:
                        v.tensor_tensor(t, t, A1r[:, ds(2 * u, 2), :], ALU.add).then_inc(fin, 1)
                        v.wait_ge(fin, n0 + 3)
                    return t, rows
                return add

            for k, bias in ((4, "gb1"), (5, "gb2")):
                plain_pass(k - 1)
                if k == 4:
                    clip_degrees(1)
                    invert_roots(1)
                rows_of = conv_rows(k, bias)
                with v.Fori(0, UNITS) as i:
                    for s in range(2):
                        u = 2 * i + s
                        v.wait_ge(projected, units_before(k, SUMS) + u + 3)
                        t, rows = rows_of(u, s)
                        v.wait_ge(row_out[s], stored(k) + 16 * i)
                        if k == 4:
                            v.tensor_tensor(rows, t, DEG[:, 0, ds(2 * u, 2)].unsqueeze(2).to_broadcast([P, 2, FEAT]),
                                            ALU.mult).then_inc(row_ok, 1)
                        else:
                            v.tensor_tensor(rows, t, X[:, ds(2 * u, 2), :], ALU.add).then_inc(row_ok, 1)

        @block.tensor
        def _(pe):
            mm = nc.tensor.matmul
            ident = res("ident")
            pe.wait_ge(s_early, 16)
            mm(BANK[7][:, 0:128], early_w("w0"), early_w("w0t"), start=True, stop=True).then_inc(s_cmm, 1)
            nr = rounds(pe)
            pe.wait_ge(s_res, 16)
            pe.wait_ge(s_cok, 1)

            def turn(k, s, u):
                pe.wait_ge(hrow_ok, u + 3)
                pe.wait_ge(ht_ok, u + 1)
                for b in range(2):
                    last = nc.tensor.transpose(BANK[2 + s][:, 128 * b:128 * b + 128], hrow[:, s, b, :], ident)
                last.then_inc(turned, 1)

            with pe.Fori(0, UNITS) as i:
                for s in range(2):
                    u = 2 * i + s
                    turn(0, s, u)
                    pe.wait_ge(ht_ok, u + 3)
                    for b in range(2):
                        pe.wait_ge(row0_a, 2 * u + b + 1)
                        pe.wait_ge(row0_v, 2 * u + b + 1)
                        mm(BANK[4 + 2 * b][:, :], hT[:, s, b, :], wall[:, 0:512], start=True, stop=True)
                        mm(BANK[5 + 2 * b][:, :], hT[:, s, b, :], wall[:, 512:1024], start=True, stop=True).then_inc(made0, 1)

            def plain_pass(p):
                with pe.Fori(0, nr) as r:
                    with pe.Fori(0, ITS) as i:
                        n = r * ITS + i
                        for j in range(IG):
                            g = 4 * n + j
                            if p in COUNTED:
                                c = COUNTED.index(p) * GROUPS * nr + g
                                pe.wait_ge(oh_ready, c + 1)
                                pe.wait_ge(deg_ok, c + 1)
                                for t in range(GT):
                                    last = mm(BANK[6][:, 0:NB], oh[:, t, 0:P], oh[:, t, P:P + NB],
                                              start=(t == 0), stop=(t == GT - 1))
                                last.then_inc(hist_mm, 1)
                            pe.wait_ge(sel_ready[p], g + 1)
                            pe.wait_ge(acc_done[p], g + 1)
                            pe.wait_ge(rows_in[p][j], 16 * GT * (n + 1))
                            for t in range(GT):
                                last = mm(BANK[4 + j % 2][:, 0:W], ring[:, j, t, :], sel[:, j % 2, t, :],
                                          start=(t == 0), stop=(t == GT - 1))
                            last.then_inc(aggs[p], 1)

            def project(k):
                with pe.Fori(0, UNITS) as i:
                    for s in range(2):
                        u = units_before(k, SUMS) + 2 * i + s
                        pe.wait_ge(added, u + 1)
                        if k == 3:
                            pe.wait_ge(part_in[s], 16 * COPIES * (i + 1))
                            for c in range(COPIES):
                                last = mm(BANK[s][:, 0:256], ident, parts[:, s, c, :], start=(c == 0), stop=(c == COPIES - 1))
                            last.then_inc(projected, 1)
                            continue
                        pe.wait_ge(staged, units_before(k, STAGED) + 2 * i + s + 3)
                        for b in range(2):
                            to = BANK[s][:, 128 * b:128 * b + 128]
                            half = stage[:, s, 0, 128 * b:128 * b + 128]
                            if k == 1:
                                last = nc.tensor.transpose(to, half, ident)
                            elif k == 2:
                                mm(to, half, res("woa"), start=True, stop=False)
                                last = mm(to, stage[:, s, 1, 128 * b:128 * b + 128], res("wob"), start=False, stop=True)
                            else:
                                last = mm(to, half, res("g1" if k == 4 else "g2"), start=True, stop=True)
                        last.then_inc(projected, 1)

            def table(k, weights):
                with pe.Fori(0, UNITS) as i:
                    for s in range(2):
                        u = units_before(k, HROWS) + 2 * i + s
                        w = units_before(k, (1, 2)) + 2 * i + s
                        turn(k, s, u)
                        pe.wait_ge(ht_ok, u + 3)
                        pe.wait_ge(row_ok, units_before(k, ROWS) + 2 * i + s + 1)
                        for b in range(2):
                            last = mm(BANK[4 + s][:, 128 * b:128 * b + 128], hT[:, s, b, :], weights, start=True, stop=True)
                        last.then_inc(made, 1)

            plain_pass(0)
            project(1)
            table(1, res("wup"))

            def first_hidden(n, j):
                g = 4 * n + j
                if j == 0:
                    pe.wait_ge(emb_in, 16 * (n + 1))
                pe.wait_ge(h1_ok, g + 1)
                mm(BANK[0][:, :], res("ew")[:, 128 * j:128 * j + 128], emb, start=True, stop=True).then_inc(h1_mm, 1)

            def second_hidden(g):
                pe.wait_ge(h1_ok, g + 2)
                pe.wait_ge(h2_ok, g + 1)
                mm(BANK[1][:, :], res("w1b"), h1, start=True, stop=True).then_inc(h2_mm, 1)

            def bias_mm(to, k):
                return mm(to, ONES[:, :], B2S[:, k, :], start=False, stop=True)

            def weights1(g, s):
                m = 2 * g + s
                if s == 0:
                    pe.wait_ge(h2_ok, g + 2)
                pe.wait_ge(msg_ok[0], m + 7)
                for t in range(4):
                    to = BANK[2 + s][:, 128 * t:128 * t + 128]
                    mm(to, h2[:, 128 * t:128 * t + 128], res("w2p")[:, 128 * s:128 * s + 128], start=True, stop=False)
                    last = bias_mm(to, 0)
                last.then_inc(w_mm, 1)

            def sums1(j, g, s):
                m = 2 * g + s
                if s == 0:
                    pe.wait_ge(sel_ready[1], g + 1)
                    pe.wait_ge(acc_done[1], g + 1)
                pe.wait_ge(msg_ok[0], m + 9)
                for a in range(2):
                    for t in range(4):
                        last = mm(BANK[4 + 2 * a + j % 2][:, 0:W], msg1[:, s, t, 128 * a:128 * a + 128],
                                  sel[:, j % 2, 4 * s + t, :], start=(s == 0 and t == 0), stop=(s == 1 and t == 3))
                last.then_inc(aggs[1], 1)

            pe.wait_ge(emb_pad, 1)
            with pe.Fori(0, nr) as r:
                def turn1(n, is_last):
                    for j in range(IG):
                        g = 4 * n + j
                        more = j + 1 < IG or not is_last
                        if more:
                            second_hidden(g + 1)
                        for s in range(2):
                            sums1(j, g, s)
                            if more:
                                weights1(g + 1, s)
                            if s == 0 and (j + 2 < IG or not is_last):
                                first_hidden(n + (j + 2) // IG, (j + 2) % IG)

                n0 = r * ITS
                first_hidden(n0, 0)
                second_hidden(4 * n0)
                first_hidden(n0, 1)
                weights1(4 * n0, 0)
                weights1(4 * n0, 1)
                with pe.Fori(0, ITS - 1) as i:
                    turn1(n0 + i, False)
                turn1(n0 + ITS - 1, True)

            project(2)
            table(2, res("wlt"))

            def inner2(n, q):
                m, j, s = 8 * n + q, q // 2, q % 2
                if s == 0:
                    pe.wait_ge(rbf_in[j % 2], 64 * (2 * n + j // 2 + 1))
                pe.wait_ge(c_ok, m + 1)
                mm(BANK[s][:, :], CW[:, :], rbf_t[:, j % 2, 512 * s:512 * s + 512], start=True, stop=True).then_inc(c_mm, 1)

            def outer2(n, q):
                m, s = 8 * n + q, q % 2
                pe.wait_ge(c_ok, m + 3)
                pe.wait_ge(m_cp, m + 1)
                for t in range(4):
                    to = BANK[2 + s][:, 128 * t:128 * t + 128]
                    mm(to, hs2[:, s, 128 * t:128 * t + 128], res("w2t"), start=True, stop=False)
                    last = bias_mm(to, 1)
                last.then_inc(m_mm, 1)

            def rows2(n, q):
                m, j, s = 8 * n + q, q // 2, q % 2
                if s == 0:
                    pe.wait_ge(pick_ok, 4 * n + j + 1)
                pe.wait_ge(msg_ok[1], m + 7)
                for t in range(4):
                    last = mm(BANK[4 + s][:, 128 * t:128 * t + 128], pick[:, j % 2, 128 * (4 * s + t):128 * (4 * s + t + 1)],
                              twin[:, j % 2, :], start=True, stop=True)
                last.then_inc(rows_mm, 1)

            def equal2(n, q):
                m, j, s = 8 * n + q, q // 2, q % 2
                if s == 0:
                    pe.wait_ge(same_ok, 4 * n + j + 4)
                pe.wait_ge(scat_ok, m + 1)
                pe.wait_ge(msg_ok[1], m + 9)
                for t in range(4):
                    last = mm(BANK[6 + s][:, 128 * t:128 * t + 128], same[:, j % 2, 4 * s + t, :], msg2[:, s, t, :],
                              start=True, stop=True)
                last.then_inc(comb_mm, 1)

            with pe.Fori(0, nr) as r:
                def turn2(n, is_last):
                    for q in range(2 * IG):
                        after = (n, q + 1) if q + 1 < 2 * IG else (n + 1, 0)
                        more = q + 1 < 2 * IG or not is_last
                        if more:
                            inner2(*after)
                        outer2(n, q)
                        if more:
                            rows2(*after)
                        if q:
                            equal2(n, q - 1)
                    equal2(n, 2 * IG - 1)

                n0 = r * ITS
                inner2(n0, 0)
                rows2(n0, 0)
                with pe.Fori(0, ITS - 1) as i:
                    turn2(n0 + i, False)
                turn2(n0 + ITS - 1, True)

            project(3)
            plain_pass(3)
            project(4)
            plain_pass(4)
            project(5)


def _laid_out(inputs):
    import numpy as np
    a = {k: np.asarray(v) for k, v in inputs.items()}
    slots = TILES * P

    def edges(array, fill):
        full = np.full((slots,) + array.shape[1:], fill, array.dtype)
        full[:EDGES] = array
        return full.reshape((TILES, P) + array.shape[1:])

    x = np.zeros((NB, P, FEAT), np.float32)
    x.reshape(NP, FEAT)[:NODES] = a["x"]
    src = edges(a["src"].astype(np.int32), NODES).reshape(ITS, IT, P).transpose(0, 2, 1)
    dst = edges(a["dst"].astype(np.int32), NODES).T
    srcl = edges(a["src"].astype(np.int32), NODES).reshape(LIN, 2 * GT * P)
    dstl = edges(a["dst"].astype(np.int32), NODES).reshape(LIN, 2 * GT * P)
    etype = edges(a["edge_type_8"].astype(np.int32), 0).T
    eweight = edges(a["edge_weight"], 0).T
    evec = edges(a["edge_attr_3"], 0).transpose(1, 0, 2).reshape(P, 3 * TILES)
    rad = np.zeros((2 * UNITS, IG, 2, 512), np.float32)
    rad.reshape(-1)[:EDGES] = a["edge_weight"]
    rad = rad.reshape(2, UNITS, IG, 2, 512).transpose(0, 2, 3, 1, 4).reshape(2 * IG * 2, UNITS * 512)
    radii = np.repeat(rad, CENTERS, axis=0)
    rbf = edges(a["edge_attr_128"], 0).reshape(GROUPS, GT * P, FEAT).transpose(0, 2, 1)

    res = np.zeros((P, RES_N), np.float32)
    early = np.zeros((P, EARLY_N), np.float32)

    def put(name, value, rows=slice(None)):
        lo, hi = RES_AT[name]
        res[rows, lo:hi] = value

    w = np.zeros((P, 128), np.float32)
    w[:MUL, :MUL] = a["L1_gnn_W_up0"]
    for c in range(3):
        w[MUL + c::3, MUL + 32 * c:MUL + 32 * c + 32] = a["L1_gnn_W_up1"]
    put("wup", w)
    woa, wob = np.zeros((P, 128), np.float32), np.zeros((P, 128), np.float32)
    woa[0:64, 0:32] = a["L1_gnn_W_out0"]
    o1 = a["L1_gnn_W_out1"]
    woa[64:96, 32::3] = o1[0:32]
    woa[96:128, 33::3] = o1[0:32]
    wob[0:32, 34::3] = o1[0:32]
    for c in range(3):
        wob[32 + 32 * c:64 + 32 * c, 32 + c::3] = o1[32:64]
    put("woa", woa)
    put("wob", wob)
    ew = np.zeros((64, IG * 128), np.float32)
    for j in range(IG):
        for s in range(2):
            ew[16 * j + 8 * s:16 * j + 8 * s + 8, 128 * j + 64 * s:128 * j + 64 * s + 64] = a["L1_gnn_mlp_w0"]
    put("ew", ew, slice(0, 64))
    w = np.zeros((P, 128), np.float32)
    w[0:64, 0:64] = w[64:128, 64:128] = a["L1_gnn_mlp_w1"]
    put("w1b", w)
    w = np.zeros((P, 256), np.float32)
    w[0:64, 0:128] = w[64:128, 128:256] = a["L1_gnn_mlp_w2"]
    put("w2p", w)
    put("w2t", a["L2_gnn_W2"].T)
    put("wlt", a["L2_gnn_Wl"].T)
    for name, key in (("bl", "L2_gnn_bl"), ("gamma", "L2_gnn_gamma"), ("beta", "L2_gnn_beta"),
                      ("gb1", "L3_gnn_b1"), ("gb2", "L3_gnn_b2"), ("g1", "L3_gnn_W1"), ("g2", "L3_gnn_W2")):
        put(name, a[key])
    put("mb0", np.concatenate([a["L1_gnn_mlp_b0"]] * 2)[:, None])
    put("mb1", np.concatenate([a["L1_gnn_mlp_b1"]] * 2)[:, None])
    put("cb0", a["L2_gnn_b0"][:, None])
    put("ident", np.eye(P, dtype=np.float32))
    put("ncen", -(np.arange(P) % CENTERS).astype(np.float32)[:, None])
    put("rowm", np.eye(3, dtype=np.float32), slice(0, 3))
    put("rowno", np.arange(P, dtype=np.float32)[:, None])
    put("eps", EPS)

    def put_early(name, value):
        lo, hi = EARLY_AT[name]
        early[:, lo:hi] = value

    put_early("bases", a["L0_gnn_bases"].transpose(1, 0, 2).reshape(P, -1))
    put_early("wcomp", a["L0_gnn_w_comp"].reshape(1, -1))
    put_early("w0", a["L2_gnn_W0"])
    put_early("w0t", a["L2_gnn_W0"].T)
    put_early("b2a", a["L1_gnn_mlp_b2"])
    put_early("b2b", a["L2_gnn_b2"])
    put_early("iota", np.arange(128, dtype=np.float32))
    put_early("before", np.tri(P, k=-1, dtype=np.float32))
    put_early("kvec", W * np.arange(1, KV + 1, dtype=np.float32))
    out = dict(x=x, src=src, dst=dst, srcl=srcl, dstl=dstl, etype=etype, eweight=eweight, radii=radii, evec=evec, rbf=rbf,
               resident=res, early=early)
    return {k: np.ascontiguousarray(v) for k, v in out.items()}


def kernel(**inputs):
    import numpy as _np
    import concourse.bacc as _bacc
    from concourse import mybir as _mybir
    from concourse.bass_utils import run_bass_kernel_spmd as _run

    nc = _bacc.Bacc("TRN2", target_bir_lowering=False, num_devices=1)
    laid = _laid_out(inputs)
    args = [nc.dram_tensor(f"in_{k}", v.shape, _mybir.dt.from_np(v.dtype), kind="ExternalInput").ap()
            for k, v in laid.items()]
    args.append(nc.dram_tensor("out_0", (NP, FEAT), _mybir.dt.float32, kind="ExternalOutput").ap())
    gnn_kernel(nc, *args)
    r = _run(nc, [{f"in_{k}": v for k, v in laid.items()}], core_ids=[0])
    return _np.asarray(r.results[0]["out_0"])[:NODES]
```

```python
import concourse.bass as bass
from concourse import mybir
from contextlib import ExitStack

P = 128
NODES = 12500
EDGES = 200000
FEAT = 128
RELS = 8
BASES = 4
MUL = 32
CENTERS = 8
GT = 8
IG = 4
IT = GT * IG
ITS = -(-EDGES // (P * IT))
GROUPS = ITS * IG
TILES = GROUPS * GT
W = 80
UNITS = 25
UB = 4
UN = UB * P
NB = UB * UNITS
NP = NB * P
KV = -(-NP // W)
ADDR_MAX = NP - W
EPS = 1e-5
PARTS = 4
COPIES = 4
SPARE = NP - P
LIN = GROUPS // 2
X_PARTS = ((0, 24), (24, 52), (52, 76), (76, NB))

RES = dict(wup=128, woa=128, wob=128, ew=IG * 128, w1b=128, w2p=256, w2t=128, wlt=128,
           bl=128, gamma=128, beta=128, g1=128, g2=128, gb1=128, gb2=128,
           ident=128, mb0=1, mb1=1, cb0=1, ncen=1, rowm=3, rowno=1, eps=1)
EARLY = dict(bases=BASES * 128, wcomp=RELS * BASES, w0=128, w0t=128, b2a=128, b2b=128, kvec=KV, iota=128, before=128)


def offsets(table):
    at, out = 0, {}
    for name, n in table.items():
        out[name] = (at, at + n)
        at += n
    return out, at


RES_AT, RES_N = offsets(RES)
EARLY_AT, EARLY_N = offsets(EARLY)
EARLY_FROM = 3072


def gnn_kernel(nc, x, src, dst, srcl, dstl, etype, eweight, radii, evec, rbf, resident, early, out):
    fp32 = mybir.dt.float32
    bf16 = mybir.dt.bfloat16
    i32 = mybir.dt.int32
    ALU = mybir.AluOpType
    ACT = mybir.ActivationFunctionType
    AX = mybir.AxisListType
    MAX = bass.bass_isa.ReduceOp.max
    ds = bass.ds

    tab0 = nc.dram_tensor("tab0", [NP * RELS, FEAT], fp32).ap()
    tabs = [tab0] + [nc.dram_tensor(f"tab{p}", [NP, FEAT], fp32).ap() for p in range(1, 5)]
    idx0 = nc.dram_tensor("idx0", [ITS, P, IT], i32).ap()
    emb_d = nc.dram_tensor("emb_d", [ITS, 64, 512], fp32).ap()
    y_d = nc.dram_tensor("y_d", [ITS, P, 3 * IT], fp32).ap()
    i16 = mybir.dt.int16
    srow_d = nc.dram_tensor("srow_d", [GROUPS, GT * P], i16).ap()
    drow_d = nc.dram_tensor("drow_d", [GROUPS, GT * P], i16).ap()
    sidx = nc.dram_tensor("sidx", [ITS, P, IT], i32).ap()
    accs = [nc.dram_tensor(f"acc{c}", [NP, FEAT], fp32).ap() for c in range(COPIES)]

    ctx = ExitStack()
    with ctx:
        def sb(name, shape, dt=fp32):
            return ctx.enter_context(nc.sbuf_tensor(name, shape, dt))

        def sem(name):
            return ctx.enter_context(nc.semaphore(name))

        X = sb("X", [P, NB, FEAT])
        A0 = sb("A0", [P, NP])
        A1 = sb("A1", [P, NP])
        WORK = sb("WORK", [P, 9568])
        R = sb("R", [P, RES_N])
        DREL = sb("DREL", [P, TILES])
        CW = sb("CW", [P, 128])
        B2S = sb("B2S", [P, 2, 128], bf16)
        ONES = sb("ONES", [P, 128], bf16)
        IOB = sb("IOB", [P, 128], bf16)
        IDX = sb("IDX", [P, 2, IT // 2], i32)
        DEG = sb("DEG", [P, 2, NB])
        ADDR0 = sb("ADDR0", [1, GROUPS], i32)
        ADDR = sb("ADDR", [1, GROUPS], i32)
        NRI = sb("NRI", [1, 1], i32)
        NRW = sb("NRW", [P, 1])
        NODE = sb("NODE", [P, 1])
        BANK = [ctx.enter_context(nc.psum_tensor(f"BANK{b}", [P, 512], fp32)) for b in range(8)]

        def res(name, rows=P):
            a, b = RES_AT[name]
            return R[0:rows, a:b]

        def work(at, n, rows=P):
            return WORK[0:rows, at:at + n]

        def early_w(name, rows=P):
            a, b = EARLY_AT[name]
            return work(EARLY_FROM + a, b - a, rows)

        ring = work(0, 4096).rearrange("p (g t f) -> p g t f", g=IG, t=GT)
        sel = work(4096, 2 * GT * W).rearrange("p (s t w) -> p s t w", s=2, t=GT)
        oh = work(5376, GT * 114).bitcast(bf16).rearrange("p (t n) -> p t n", t=GT)
        msg1 = work(5376, 2048).rearrange("p (s t f) -> p s t f", s=2, t=4)
        h1 = work(7424, 512)
        h2 = work(7936, 512)
        emb = work(8448, 512)
        scals = work(8960, 256).rearrange("p (s t m) -> p s t m", s=2, t=4)
        ubufs = work(9216, 256).rearrange("p (s t m) -> p s t m", s=2, t=4)
        ybuf = work(9472, 96).rearrange("p (h t c) -> p h t c", h=2, c=3)
        srow0 = work(7200, 1024).bitcast(i16).rearrange("p (s n) -> p s n", s=2)
        rbuf = work(6400, 512, 64)
        ebuf = work(8736, 512, 64)
        vbuf = work(9248, 3 * IT).rearrange("p (t c) -> p t c", c=3)
        vsq = work(9248 + 3 * IT, 3 * IT).rearrange("p (t c) -> p t c", c=3)
        vlen = work(9248 + 6 * IT, IT)
        same0 = work(8224, 512).bitcast(bf16).rearrange("p (t e) -> p t e", t=GT)
        dsts_i = work(4096, TILES).bitcast(i32)
        dpart_i = work(4096 + TILES, TILES).bitcast(i32)
        dst_bits = work(4096 + 2 * TILES, TILES).bitcast(bf16).rearrange("p (k n) -> p k n", k=2)
        rbf_t = A0[:, 0:2048].rearrange("p (s n) -> p s n", s=2)
        srow = A0[:, 2048:3072].bitcast(i16).rearrange("p (s n) -> p s n", s=2)
        drow = A0[:, 3072:4096].bitcast(i16).rearrange("p (s n) -> p s n", s=2)
        twin = A0[:, 4096:4352].rearrange("p (s f) -> p s f", s=2)
        pick = A0[:, 4352:6400].rearrange("p (s n) -> p s n", s=2)
        same = A0[:, 6400:8448].rearrange("p (s t e) -> p s t e", s=2, t=GT)
        hs2 = A0[:, 8448:9472].rearrange("p (s n) -> p s n", s=2)
        mout = A0[:, 9472:10496].rearrange("p (s n) -> p s n", s=2)
        msg2 = A0[:, 10496:11520].rearrange("p (s t f) -> p s t f", s=2, t=4)
        srcc = A0[:, 11520:11552].bitcast(i32)
        parts = A0[:, 0:PARTS * COPIES * UN].rearrange("p (s c n) -> p s c n", s=PARTS, c=COPIES)
        stage = work(0, 4 * UN).rearrange("p (s a n) -> p s a n", s=2, a=2)
        hrow = work(2048, 2 * UN).rearrange("p (s b f) -> p s b f", s=2, b=UB)
        hT = work(3072, 2 * UN).rearrange("p (s b f) -> p s b f", s=2, b=UB)
        trow = work(4096, 2 * UN).rearrange("p (s b f) -> p s b f", s=2, b=UB)
        stat = work(5120, 6 * NB).rearrange("p (b c) -> p b c", c=6)
        rstd = work(5720, NB)
        nmr = work(5820, NB)
        mean = work(5920, NB)
        var = work(6020, NB)
        dif = work(6120, NB)
        t0row = work(7264, 2048).rearrange("p (s n) -> p s n", s=2)
        wall = work(6220, RELS * 128)
        gmin = work(8704, GROUPS)
        base = work(8900, GROUPS)
        dmax = work(9096, 2)
        kcmp = work(9100, KV)
        b2f = work(9264, 128)

        A1b = A1[:, :].bitcast(bf16)
        dst_i = A0[:, 0:TILES].bitcast(i32)
        typ_i = A0[:, 2 * TILES:3 * TILES].bitcast(i32)
        idx_i = A0[:, 3 * TILES:4 * TILES].bitcast(i32)
        ew_t = A1[:, 0:TILES]
        src_bits = A1b[:, 2 * TILES:4 * TILES].rearrange("p (k n) -> p k n", k=2)
        srcs_i = A1[:, 3 * TILES:4 * TILES].bitcast(i32)
        part_i = A1[:, 5 * TILES:6 * TILES].bitcast(i32)
        earlier = A1[:, 5 * TILES:6 * TILES]
        sidx_f = A1[:, 6 * TILES:7 * TILES]
        sidx_i = A1[:, 7 * TILES:8 * TILES].bitcast(i32)
        beforeb = A1b[:, 25088:25088 + 128]
        dstl_i = A0[0:LIN, 4 * TILES:4 * TILES + 2048].bitcast(i32)
        srcl_i = A0[0:LIN, 4 * TILES + 2048:4 * TILES + 4096].bitcast(i32)
        low = A0[0:LIN, 4 * TILES + 4096:4 * TILES + 4098]
        dstl_s = A0[0:LIN, 11000:11000 + 1024].bitcast(i16)
        srcl_s = A1[0:LIN, 6 * TILES:6 * TILES + 1024].bitcast(i16)

        s_res = sem("s_res")
        s_early = sem("s_early")
        s_x = [sem(f"s_x{c}") for c in range(4)]
        s_dst, s_src, s_typ = sem("s_dst"), sem("s_src"), sem("s_typ")
        s_ewt, s_dsts = sem("s_ewt"), sem("s_dsts")
        s_idxc, s_idx0 = sem("s_idxc"), sem("s_idx0")
        chain = sem("chain")
        s_gmin, s_gall, s_dmax, s_dall, s_nr = (sem(n) for n in ("s_gmin", "s_gall", "s_dmax", "s_dall", "s_nr"))
        s_cmm, s_cok, s_ew = sem("s_cmm"), sem("s_cok"), sem("s_ew")
        s_zero0 = [sem(f"s_zero0{p}") for p in range(5)]
        s_zero1 = sem("s_zero1")
        s_deg, s_degr = sem("s_deg"), sem("s_degr")

        GATHER = (0, 1, 3, 4)
        COUNTED = (0, 3)
        rows_in = {p: [sem(f"rows_in{p}{j}") for j in range(IG)] for p in GATHER}
        idx_in = [sem(f"idx_in{h}") for h in range(2)]
        sel_ready = {p: sem(f"sel_ready{p}") for p in GATHER}
        aggs = {p: sem(f"aggs{p}") for p in GATHER}
        acc_done = {p: sem(f"acc_done{p}") for p in GATHER}
        moved = [sem(f"moved{p}") for p in range(5)]
        oh_ready, hist_mm, deg_ok, deg_zero = (sem(n) for n in ("oh_ready", "hist_mm", "deg_ok", "deg_zero"))
        vec_in, y_step, len_ok, root_ok, y_ok, y_out = (
            sem(n) for n in ("vec_in", "y_step", "len_ok", "root_ok", "y_ok", "y_out"))
        rad_in, clip_ok, square_ok, exp_ok, emb_ok, emb_out = (
            sem(n) for n in ("rad_in", "clip_ok", "square_ok", "exp_ok", "emb_ok", "emb_out"))
        emb_in = sem("emb_in")
        y_in = [sem(f"y_in{h}") for h in range(2)]
        h1_mm, h1_ok, h2_mm, h2_ok, w_mm = (sem(n) for n in ("h1_mm", "h1_ok", "h2_mm", "h2_ok", "w_mm"))
        s_wsel, s_t, s_scal, s_u = (sem(n) for n in ("s_wsel", "s_t", "s_scal", "s_u"))
        emb_pad = sem("emb_pad")
        s_dstl, s_srcl, s_rows16, s_rows_out, s_sidx, s_sidx_out = (
            sem(n) for n in ("s_dstl", "s_srcl", "s_rows16", "s_rows_out", "s_sidx", "s_sidx_out"))
        srow0_in = [sem(f"srow0_in{k}") for k in range(2)]
        same0_ok = sem("same0_ok")
        zero_out = sem("zero_out")
        pick_ok, same_ok, rows_mm, m_cp, comb_mm, scat_ok = (
            sem(n) for n in ("pick_ok", "same_ok", "rows_mm", "m_cp", "comb_mm", "scat_ok"))
        scat = [sem(f"scat{c}") for c in range(COPIES)]
        ring_free = sem("ring_free")
        srcc_in = [sem(f"srcc_in{h}") for h in range(2)]
        part_in = [sem(f"part_in{s}") for s in range(PARTS)]
        msg_ok = [sem(f"msg_ok{p}") for p in range(2)]
        rbf_in = [sem(f"rbf_in{s}") for s in range(2)]
        c_mm, c_ok, m_mm = sem("c_mm"), sem("c_ok"), sem("m_mm")

        staged, projected, added, stats = (sem(n) for n in ("staged", "projected", "added", "stats"))
        s_var, s_sd, s_norm = sem("s_var"), sem("s_sd"), sem("s_norm")
        hrow_ok, turned, ht_ok, made, row_ok = (sem(n) for n in ("hrow_ok", "turned", "ht_ok", "made", "row_ok"))
        made0, row0_a, row0_v = sem("made0"), sem("row0_a"), sem("row0_v")
        normed, scaled, affine, keep_ok = sem("normed"), sem("scaled"), sem("affine"), sem("keep_ok")
        fin = sem("fin")
        row_out = [sem(f"row_out{s}") for s in range(2)]

        carried = sem("carried")
        credits = [(staged, 2), (projected, 2), (added, 2), (hrow_ok, 2), (turned, 2), (ht_ok, 2), (made, 2),
                   (row_ok, 2), (made0, UB + 1), (row0_a, 2), (row0_v, 2), (hist_mm, 1), (deg_ok, 1),
                   (h1_mm, 1), (h1_ok, 1), (h2_mm, 1), (h2_ok, 1), (w_mm, 1), (c_mm, 4), (c_ok, 2), (m_mm, 2),
                   (same0_ok, 2), (rows_mm, 4), (same_ok, 3), (m_cp, 2), (comb_mm, 4), (scat_ok, 2), (ring_free, IG - 1)]
        credits += [(s, 1) for s in moved + row_out + [y_out, emb_out, emb_ok]]
        credits += [(s, 4) for s in aggs.values()] + [(s, 2) for s in acc_done.values()] + [(s, 8) for s in msg_ok]

        block = ctx.enter_context(nc.Block())

        def zeroed(nr):
            return 16 * COPIES * (ITS * nr + 1)

        def rounds(eng):
            eng.wait_ge(s_nr, 1)
            return eng.value_load(NRI[0:1, 0:1], min_val=1, max_val=KV + 1)

        def apart(eng):
            eng.sem_inc(carried, 1)

        def stored(k, s):
            tables = sum(UNITS // 2 + (s == (j + 1) % 2) for j in range(1, k))
            return 1 + (16 * (NB // 2 + tables) if k else 0)

        def slot(k, s):
            return (s + k + 1) % 2

        def turn_slot(k, s):
            return (s + k) % 2

        def each_unit(eng, body, slots=2):
            with eng.Fori(0, UNITS // slots) as i:
                for s in range(slots):
                    body(slots * i + s, s)
            for s in range(UNITS % slots):
                body(UNITS - UNITS % slots + s, s)

        def ahead(eng, by, first, second, slots=2):
            for u in range(by):
                first(u, u % slots)
            turns = (UNITS - by) // slots
            with eng.Fori(0, turns) as i:
                for s in range(slots):
                    first(slots * i + s + by, (s + by) % slots)
                    second(slots * i + s, s)
            for u in range(slots * turns, UNITS):
                if u + by < UNITS:
                    first(u + by, (u + by) % slots)
                second(u, u % slots)

        def units_before(k, stages):
            return UNITS * sum(1 for j in stages if j < k)

        SUMS = (1, 2, 3, 4, 5)
        STAGED = (1, 2, 4, 5)
        HROWS = (0, 1, 2)
        ROWS = (1, 2, 3, 4, 5)

        @block.sync
        def _(sp):
            sp.dma_start(dst_i, dst).then_inc(s_dst, 16)
            sp.dma_start(work(EARLY_FROM, EARLY_N), early).then_inc(s_early, 16)
            for c, (lo, hi) in enumerate(X_PARTS):
                sp.dma_start(X[:, lo:hi, :], x[lo:hi].rearrange("b p f -> p b f")).then_inc(s_x[c], 16)
            sp.dma_start(dstl_i, dstl).then_inc(s_dstl, 16)
            sp.dma_start(srcl_i, srcl).then_inc(s_srcl, 16)
            sp.dma_start(srcs_i.rearrange("p (i t) -> p i t", t=IT), src.rearrange("i p t -> p i t")).then_inc(s_src, 16)
            sp.dma_start(typ_i, etype).then_inc(s_typ, 16)
            sp.dma_start(ew_t, eweight).then_inc(s_ewt, 16)
            sp.wait_ge(s_rows16, 2)
            sp.dma_start(drow_d.rearrange("(p g) n -> p (g n)", g=2), dstl_s).then_inc(s_rows_out, 16)
            sp.dma_start(srow_d.rearrange("(p g) n -> p (g n)", g=2), srcl_s).then_inc(s_rows_out, 16)
            sp.wait_ge(s_idxc, 1)
            sp.dma_start(idx0.rearrange("i p t -> p i t"), idx_i.rearrange("p (i t) -> p i t", t=IT)).then_inc(s_idx0, 16)

            tab0_v = tab0.rearrange("(b p r) f -> b p (r f)", p=P, r=RELS)
            with sp.Fori(0, NB // 2) as i:
                for s in range(2):
                    sp.wait_ge(row0_a, 2 * i + s + 3)
                    sp.wait_ge(row0_v, 2 * i + s + 3)
                    sp.dma_start(tab0_v[ds(2 * i + s, 1)].rearrange("b p f -> (b p) f"), t0row[:, s])\
                      .then_inc(row_out[s], 16)

            nr = rounds(sp)
            def store_rows(k, table):
                view = table.rearrange("(b p) f -> b p f", p=P)

                def store(u, s):
                    s = slot(k, s)
                    sp.wait_ge(row_ok, units_before(k, ROWS) + u + 3)
                    sp.dma_start(view[ds(UB * u, UB)].rearrange("b p f -> p b f"), trow[:, s]).then_inc(row_out[s], 16)

                each_unit(sp, store)

            def load_indices(p, h, i, n):
                if p == 1:
                    sp.wait_ge(msg_ok[0], 8 * n + 4 * h + 4)
                else:
                    sp.wait_ge(aggs[p], 4 * n + 2 * h + 2)
                apart(sp)
                sp.dma_start(IDX[:, h, :], (idx0 if p == 0 else src)[ds(i, 1), :, 16 * h:16 * h + 16]
                             .rearrange("a p t -> (a p) t")).then_inc(idx_in[h], 16)

            def index_pass(p):
                with sp.Fori(0, nr) as r:
                    with sp.Fori(0, ITS) as i:
                        n = r * ITS + i
                        for h in range(2):
                            load_indices(p, h, i, n)
                            for k in range(2 if p == 0 else 0):
                                g = 4 * n + 2 * h + k
                                sp.wait_ge(same0_ok, g + 1)
                                sp.dma_start(srow0[:, k], srow_d[ds(4 * i + 2 * h + k, 1), :].to_broadcast([P, GT * P]))\
                                  .then_inc(srow0_in[k], 16)
                            if p == 0 and h == 0:
                                sp.wait_ge(y_out, 16 * n + 1)
                                sp.dma_start(vbuf.rearrange("p t c -> p (t c)"), evec[:, ds(3 * IT * i, 3 * IT)])\
                                  .then_inc(vec_in, 16)
                                sp.wait_ge(emb_ok, n + 1)
                                sp.dma_start(rbuf, radii[ds(i, 1)].rearrange("a q n -> (a q) n")).then_inc(rad_in, 16)
                        if p == 0:
                            sp.wait_ge(y_ok, n + 1)
                            sp.dma_start(y_d[ds(i, 1)].rearrange("a p t -> (a p) t"), vbuf.rearrange("p t c -> p (t c)"))\
                              .then_inc(y_out, 16)
                            sp.wait_ge(emb_ok, n + 2)
                            sp.dma_start(emb_d[ds(i, 1)].rearrange("a q n -> (a q) n"), ebuf).then_inc(emb_out, 16)

            for s in range(2):
                sp.wait_ge(row_out[s], stored(1, s))
            sp.wait_ge(s_idx0, 16)
            sp.wait_ge(s_rows_out, 32)
            index_pass(0)
            sp.wait_ge(s_sidx, 1)
            sp.dma_start(sidx.rearrange("i p t -> p i t"), sidx_i.rearrange("p (i t) -> p i t", t=IT)).then_inc(s_sidx_out, 16)
            store_rows(1, tabs[1])
            for s in range(2):
                sp.wait_ge(row_out[s], stored(2, s))
            def zero_sums(i):
                for acc in accs:
                    sp.dma_start(acc.rearrange("(i q n) f -> i q (n f)", i=ITS + 1, q=64)[ds(i, 1)]
                                 .rearrange("a q n -> (a q) n"), emb[64:128, :]).then_inc(zero_out, 16)

            sp.wait_ge(emb_pad, 1)
            sp.wait_ge(y_out, 16 * ITS * nr + 1)
            apart(sp)
            sp.wait_ge(emb_out, 16 * ITS * nr + 1)
            apart(sp)
            with sp.Fori(0, nr) as r:
                with sp.Fori(0, ITS) as i:
                    n = r * ITS + i
                    load_indices(1, 0, i, n)
                    sp.wait_ge(h1_mm, 4 * n + 1)
                    sp.dma_start(emb[0:64, :], emb_d[ds(i, 1)].rearrange("a q n -> (a q) n")).then_inc(emb_in, 16)
                    for h in range(2):
                        if h == 1:
                            load_indices(1, 1, i, n)
                        sp.wait_ge(msg_ok[0], 8 * n + 4 * h + 4)
                        sp.dma_start(ybuf[:, h].rearrange("p t c -> p (t c)"),
                                     y_d[ds(i, 1), :, 48 * h:48 * h + 48].rearrange("a p t -> (a p) t"))\
                          .then_inc(y_in[h], 16)
                    zero_sums(i)
            zero_sums(ITS)
            store_rows(2, tabs[2])
            sp.wait_ge(s_zero0[2], 1)
            for s in range(2):
                sp.wait_ge(row_out[s], stored(3, s))
            sp.dma_start(dsts_i, dst).then_inc(s_dsts, 16)
            with sp.Fori(0, nr) as r:
                sp.wait_ge(moved[2], 2 * r + 1)
                apart(sp)
                with sp.Fori(0, ITS) as i:
                    n = r * ITS + i
                    for j in range(IG):
                        g, h, k = 4 * n + j, j // 2, j % 2
                        if k == 0:
                            sp.wait_ge(same_ok, 4 * n + 2 * h + 1)
                            sp.dma_start(srcc[:, 16 * h:16 * h + 16], src[ds(i, 1), :, 16 * h:16 * h + 16]
                                         .rearrange("a p t -> (a p) t")).then_inc(srcc_in[h], 16)
                        start = sp.value_load(ADDR[0:1, ds(4 * i + j, 1)], min_val=0, max_val=ADDR_MAX)
                        sp.wait_ge(rows_mm, 2 * g + 2)
                        apart(sp)
                        sp.wait_ge(same_ok, g + 2)
                        sp.dma_start(rbf_t[:, k], rbf[ds(4 * i + j, 1)].rearrange("a p n -> (a p) n")).then_inc(rbf_in[k], 16)
                        sp.dma_start(srow[:, k], srow_d[ds(4 * i + j, 1), :].to_broadcast([P, GT * P])).then_inc(rbf_in[k], 16)
                        sp.dma_start(drow[0:W, k], drow_d[ds(4 * i + j, 1), :].to_broadcast([W, GT * P])).then_inc(rbf_in[k], 16)
                        sp.dma_start(twin[0:W, k], tabs[2][ds(start, W), :]).then_inc(rbf_in[k], 16)
                        if k == 1:
                            sp.wait_ge(ring_free, 4 * n + 2 * h + 2)
                            sp.dma_start(IDX[:, h, :], sidx[ds(i, 1), :, 16 * h:16 * h + 16]
                                         .rearrange("a p t -> (a p) t")).then_inc(idx_in[h], 16)
            for c in range(COPIES):
                sp.wait_ge(scat[c], 16 * 2 * GROUPS * nr)
                apart(sp)

            def load_parts(u, s):
                sp.wait_ge(added, units_before(3, SUMS) + u + 3 - PARTS)
                for c, acc in enumerate(accs):
                    sp.dma_start(parts[:, s, c, :].rearrange("p (b f) -> p b f", b=UB),
                                 acc.rearrange("(b p) f -> b p f", p=P)[ds(UB * u, UB)]
                                 .rearrange("b p f -> p b f")).then_inc(part_in[s], 16)

            each_unit(sp, load_parts, PARTS)
            store_rows(3, tabs[3])
            index_pass(3)
            store_rows(4, tabs[4])
            index_pass(4)
            store_rows(5, out)
            for s in range(2):
                sp.wait_ge(row_out[s], stored(6, s))

        @block.gpsimd
        def _(pool):
            pool.wait_ge(s_gmin, 1)
            pool.partition_all_reduce(base, gmin, P, MAX).then_inc(s_gall, 1)
            pool.wait_ge(s_dmax, 1)
            pool.partition_all_reduce(dmax[:, 1:2], dmax[:, 0:1], P, MAX).then_inc(s_dall, 1)
            nr = rounds(pool)
            pool.wait_ge(s_idx0, 16)
            pool.wait_ge(s_rows_out, 32)
            pool.memset(A0[:, :], 0.0).then_inc(s_zero0[0], 1)

            def scatter_pass():
                def turn2(n, is_first):
                    for j in range(IG):
                        if j % 2 == 0:
                            pool.wait_ge(idx_in[j // 2], 16 * (2 * ITS * nr + n + 1))
                        for t in range(GT):
                            if t % 4 == 0:
                                pool.wait_ge(scat_ok, 2 * (4 * n + j) + t // 4 + 3)
                            c = t % COPIES
                            if not (is_first and j == 0 and t < COPIES):
                                pool.wait_ge(scat[c], 16 * (2 * (4 * n + j) + t // COPIES))
                            if t == COPIES - 1:
                                pool.sem_inc(ring_free, 1)
                            else:
                                apart(pool)
                            col = GT * (j % 2) + t
                            pool.indirect_dma_start(accs[c], bass.IndirectOffsetOnAxis(IDX[:, j // 2, col:col + 1], 0),
                                                    ring[:, j, t, :], None, compute_op=ALU.add).then_inc(scat[c], 16)

                with pool.Fori(0, nr) as r:
                    turn2(r * ITS, True)
                    with pool.Fori(0, ITS - 1) as i:
                        turn2(r * ITS + i + 1, False)
                    for c in range(COPIES):
                        pool.wait_ge(scat[c], 16 * 2 * GROUPS * (r + 1))

            for p in range(5):
                for s in range(2):
                    pool.wait_ge(row_out[s], stored(p + 1, s))
                if p == 2:
                    pool.wait_ge(zero_out, zeroed(nr))
                    apart(pool)
                    pool.wait_ge(s_sidx_out, 16)
                    scatter_pass()
                    pool.wait_ge(added, 2 + units_before(4, SUMS))
                    pool.memset(A0[:, :], 0.0).then_inc(s_zero0[3], 1)
                    continue
                with pool.Fori(0, nr) as r:
                    with pool.Fori(0, ITS) as i:
                        n = r * ITS + i
                        for j in range(IG):
                            if j % 2 == 0:
                                pool.wait_ge(idx_in[j // 2], 16 * (p * ITS * nr + n + 1))
                            if p == 1:
                                pool.wait_ge(msg_ok[0], 2 * (4 * n + j) + 2)
                            else:
                                pool.wait_ge(aggs[p], 4 * n + j + 1)
                            apart(pool)
                            for t in range(GT):
                                c = GT * (j % 2) + t
                                pool.indirect_dma_start(ring[:, j, t, :], None, tabs[p],
                                                        bass.IndirectOffsetOnAxis(IDX[:, j // 2, c:c + 1], 0))\
                                    .then_inc(rows_in[p][j], 16)
                if p == 0:
                    pool.wait_ge(acc_done[0], 2 + GROUPS * nr)
                    apart(pool)
                    pool.wait_ge(s_sidx_out, 16)
                    pool.memset(A1[:, :], 0.0).then_inc(s_zero1, 1)
                if p < 4:
                    pool.wait_ge(staged, 2 + units_before(p + 2, STAGED))
                    pool.memset(A0[:, :], 0.0).then_inc(s_zero0[p + 1], 1)

        @block.scalar
        def _(act):
            act.dma_start(R[:, :], resident).then_inc(s_res, 16)
            act.wait_ge(s_res, 16)

            def root(which):
                act.wait_ge(s_var, which + 1)
                nc.scalar.activation(rstd, var, ACT.Sqrt, bias=res("eps")).then_inc(s_sd, 1)

            def degree_roots(k):
                act.wait_ge(s_deg, k + 1)
                nc.scalar.activation(DEG[:, k], DEG[:, k], ACT.Sqrt).then_inc(s_degr, 1)

            def stage_sums(k):
                halves = (A0, A1) if k == 2 else (A0,)

                def copy(u, s):
                    act.wait_ge(projected, units_before(k, SUMS) + u + 1)
                    for a, half in enumerate(halves):
                        last = nc.scalar.activation(stage[:, slot(k, s), a, :], half[:, ds(UN * u, UN)], ACT.Copy)
                    last.then_inc(staged, 1)

                each_unit(act, copy)

            root(0)
            act.wait_ge(s_norm, 1)

            def h_rows(k, u, s):
                act.wait_ge(turned, units_before(k, HROWS) + u + 1)
                for b in range(UB):
                    at = ds(UB * u + b, 1)
                    last = nc.scalar.activation(hrow[:, turn_slot(k, s), b, :], X[:, at, :].rearrange("p b f -> p (b f)"), ACT.Relu,
                                                bias=nmr[:, at], scale=rstd[:, at])
                last.then_inc(hrow_ok, 1)

            def half_rows0(u, s):
                for b in range(UB):
                    act.wait_ge(made0, UB * u + b + UB + 2)
                    act.wait_ge(row_out[b % 2], stored(0, 0) + 16 * (UB // 2 * u + b // 2))
                    nc.scalar.activation(t0row[:, b % 2, 0:512], BANK[4 + 2 * (b % 2)][:, :], ACT.Copy).then_inc(row0_a, 1)

            ahead(act, 2, lambda u, s: h_rows(0, u, s), half_rows0)

            nr = rounds(act)
            with act.Fori(0, nr) as r:
                with act.Fori(0, ITS) as i:
                    n = r * ITS + i
                    act.wait_ge(len_ok, n + 1)
                    nc.scalar.activation(vlen, vlen, ACT.Sqrt).then_inc(root_ok, 1)
                    act.wait_ge(clip_ok, n + 1)
                    nc.scalar.activation(ebuf, ebuf, ACT.Square, bias=res("ncen", 64), scale=float(CENTERS - 1))\
                      .then_inc(square_ok, 1)
                    act.wait_ge(square_ok, n + 1)
                    nc.scalar.activation(ebuf, ebuf, ACT.Exp, scale=-0.5).then_inc(exp_ok, 1)

            act.wait_ge(acc_done[0], 2 + GROUPS * nr)
            stage_sums(1)
            degree_roots(0)
            root(1)

            def transposed_rows(k, which):
                act.wait_ge(s_norm, which + 1)

                def rows(u, s):
                    h_rows(k, u, s)
                    if k == 2:
                        act.wait_ge(hrow_ok, units_before(k, HROWS) + u + 3)
                        nc.scalar.activation(A1[:, ds(UN * u, UN)], hrow[:, turn_slot(k, s)].rearrange("p b f -> p (b f)"),
                                             ACT.Copy).then_inc(keep_ok, 1)

                each_unit(act, rows)

            transposed_rows(1, 1)

            with act.Fori(0, nr) as r:
                with act.Fori(0, ITS) as i:
                    for j in range(IG):
                        g = 4 * (r * ITS + i) + j
                        act.wait_ge(h1_mm, g + 2)
                        act.wait_ge(h2_mm, g + 1)
                        nc.scalar.activation(h1, BANK[0][:, :], ACT.Silu, bias=res("mb0")).then_inc(h1_ok, 1)
                        act.wait_ge(h2_mm, g + 2)
                        act.wait_ge(w_mm, 2 * g + 1)
                        nc.scalar.activation(h2, BANK[1][:, :], ACT.Silu, bias=res("mb1")).then_inc(h2_ok, 1)

            act.wait_ge(acc_done[1], 2 + GROUPS * nr)
            stage_sums(2)
            root(2)
            transposed_rows(2, 2)

            def silu2(m, s):
                act.wait_ge(c_mm, m + 5)
                act.wait_ge(m_mm, m + 1)
                nc.scalar.activation(hs2[:, s], BANK[s][:, :], ACT.Silu, bias=res("cb0")).then_inc(c_ok, 1)

            def copy_m(m, s):
                act.wait_ge(m_mm, m + 3)
                act.wait_ge(msg_ok[1], m + 7)
                nc.scalar.activation(mout[:, s], BANK[2 + s][:, :], ACT.Copy).then_inc(m_cp, 1)

            def copy_sums(n, j, m, s):
                act.wait_ge(comb_mm, m + 5)
                if s == 0:
                    act.wait_ge(ring_free, 4 * n + j + 1)
                nc.scalar.activation(ring[:, j, 4 * s:4 * s + 4, :].rearrange("p t f -> p (t f)"), BANK[6 + s][:, :],
                                     ACT.Copy).then_inc(scat_ok, 1)

            act.wait_ge(s_zero0[2], 1)
            for s in range(2):
                act.wait_ge(row_out[s], stored(3, s))
            with act.Fori(0, nr) as r:
                def turn2(n, is_last):
                    for q in range(2 * IG):
                        if q + 1 < 2 * IG or not is_last:
                            silu2(8 * n + q + 1, (q + 1) % 2)
                        copy_m(8 * n + q, q % 2)
                        if q:
                            copy_sums(n, (q - 1) // 2, 8 * n + q - 1, (q - 1) % 2)
                    copy_sums(n, IG - 1, 8 * n + 2 * IG - 1, 1)

                n0 = r * ITS
                silu2(8 * n0, 0)
                with act.Fori(0, ITS - 1) as i:
                    turn2(n0 + i, False)
                turn2(n0 + ITS - 1, True)

            root(3)
            act.wait_ge(s_norm, 4)

            def own_norm(u, s):
                for b in range(UB):
                    c = UB * u + b
                    h = A1[:, ds(P * c, P)]
                    last = nc.scalar.activation(h, h, ACT.Identity, bias=nmr[:, ds(c, 1)], scale=rstd[:, ds(c, 1)])
                last.then_inc(normed, 1)

            each_unit(act, own_norm)
            root(4)
            act.wait_ge(s_norm, 5)

            def h_of_layer3(u, s):
                for b in range(UB):
                    c = UB * u + b
                    last = nc.scalar.activation(A1[:, ds(P * c, P)], X[:, ds(c, 1), :].rearrange("p b f -> p (b f)"),
                                                ACT.Relu, bias=nmr[:, ds(c, 1)], scale=rstd[:, ds(c, 1)])
                last.then_inc(normed, 1)

            each_unit(act, h_of_layer3)
            for p in (3, 4):
                act.wait_ge(acc_done[p], 2 + GROUPS * nr)
                if p == 3:
                    degree_roots(1)
                stage_sums(p + 1)

        @block.vector
        def _(v):
            done = [0]

            def step(ins):
                done[0] += 1
                ins.then_inc(chain, 1)
                v.wait_ge(chain, done[0])

            for s, n in credits:
                v.sem_inc(s, n)

            v.wait_ge(s_dst, 16)
            step(v.tensor_copy(DREL[:, :], dst_i))
            v.tensor_reduce(gmin, DREL[:, :].rearrange("p (g t) -> p g t", t=GT), AX.X, ALU.min, negate=True)\
             .then_inc(s_gmin, 1)
            v.wait_ge(s_gall, 1)
            step(v.tensor_scalar(base, base, -1.0, None, ALU.mult))
            drel_g = DREL[:, :].rearrange("p (g t) -> p g t", t=GT)
            step(v.tensor_tensor(drel_g, drel_g, base.unsqueeze(2).to_broadcast([P, GROUPS, GT]), ALU.subtract))
            step(v.tensor_copy(ADDR0[:, :], base[0:1, :]))
            step(v.tensor_copy(ADDR[:, :], ADDR0[:, :]))
            v.tensor_reduce(dmax[:, 0:1], DREL[:, :], AX.X, ALU.max).then_inc(s_dmax, 1)
            v.wait_ge(s_dall, 1)
            v.wait_ge(s_early, 16)
            step(v.tensor_scalar(kcmp, early_w("kvec"), dmax[:, 1:2], None, ALU.is_le))
            step(v.tensor_reduce(NRW[:, :], kcmp, AX.X, ALU.add))
            step(v.tensor_scalar(NRW[:, :], NRW[:, :], 1.0, None, ALU.add))
            step(v.tensor_copy(NRI[:, :], NRW[0:1, :]))
            v.tensor_scalar(NRW[:, :], NRW[:, :], float(W), None, ALU.mult).then_inc(s_nr, 1)

            v.wait_ge(s_nr, 1)
            nr = rounds(v)

            bases = early_w("bases").rearrange("p (b f) -> p b f", b=BASES)
            for rel in range(RELS):
                m = wall[:, 128 * rel:128 * rel + 128]
                for b in range(BASES):
                    k = rel * BASES + b
                    coef = early_w("wcomp")[:, k:k + 1]
                    if b == 0:
                        step(v.tensor_scalar(m, bases[:, b], coef, None, ALU.mult))
                    else:
                        step(v.scalar_tensor_tensor(out=m, in0=bases[:, b], scalar=coef, in1=m, op0=ALU.mult, op1=ALU.add))
            v.wait_ge(s_res, 16)
            step(v.tensor_copy(IOB[:, :], early_w("iota")))
            step(v.tensor_copy(NODE[:, :], res("rowno")))
            step(v.memset(ONES[:, :], 1.0))
            for k, name in enumerate(("b2a", "b2b")):
                rest = early_w(name)
                step(v.tensor_scalar(b2f, rest, res("rowm")[:, 0:1], None, ALU.mult))
                for part in (1, 2):
                    step(v.tensor_copy(B2S[:, k, :], rest))
                    step(v.tensor_tensor(rest, rest, B2S[:, k, :], ALU.subtract))
                    step(v.scalar_tensor_tensor(out=b2f, in0=rest, scalar=res("rowm")[:, part:part + 1], in1=b2f,
                                                op0=ALU.mult, op1=ALU.add))
                step(v.tensor_copy(B2S[:, k, :], b2f))
            step(v.tensor_scalar(res("ew"), res("ew"), float(CENTERS) ** 0.5, None, ALU.mult))
            v.tensor_scalar(res("woa")[32:64, :], res("woa")[32:64, :], 3.0 ** -0.5, None, ALU.mult).then_inc(s_ew, 1)
            v.wait_ge(s_cmm, 1)
            v.tensor_copy(CW[:, :], BANK[7][:, 0:128]).then_inc(s_cok, 1)

            def finish_stats(which):
                v.wait_ge(stats, UNITS * (which + 1))
                step(v.tensor_tensor(mean, stat[:, :, 1], stat[:, :, 4], ALU.add))
                step(v.tensor_tensor(dif, stat[:, :, 1], stat[:, :, 4], ALU.subtract))
                step(v.tensor_tensor(var, stat[:, :, 2], stat[:, :, 5], ALU.add))
                step(v.tensor_tensor(dif, dif, dif, ALU.mult))
                step(v.tensor_scalar(dif, dif, 0.25, None, ALU.mult))
                v.scalar_tensor_tensor(out=var, in0=var, scalar=1.0 / FEAT, in1=dif, op0=ALU.mult, op1=ALU.add)\
                 .then_inc(s_var, 1)
                v.wait_ge(s_sd, which + 1)
                step(v.reciprocal(rstd, rstd))
                v.scalar_tensor_tensor(out=nmr, in0=mean, scalar=-0.5, in1=rstd, op0=ALU.mult, op1=ALU.mult)\
                 .then_inc(s_norm, 1)

            def row_stats(rows_of, b0):
                for b in range(UB):
                    at = ds(b0 + b, 1)
                    last = v.bn_stats(stat[:, at, :].rearrange("p b c -> p (b c)"), rows_of(b))
                last.then_inc(stats, 1)

            def x_block(c):
                return X[:, ds(c, 1), :].rearrange("p b f -> p (b f)")

            for c, (lo, hi) in enumerate(X_PARTS):
                v.wait_ge(s_x[c], 16)
                with v.Fori(lo // UB, hi // UB) as u:
                    row_stats(lambda b: x_block(UB * u + b), UB * u)

            v.wait_ge(s_dstl, 16)
            lin = dstl_i.rearrange("p (g n) -> p g n", g=2)
            step(v.tensor_reduce(low, lin, AX.X, ALU.min))
            v.tensor_tensor(dstl_s.rearrange("p (g n) -> p g n", g=2), lin,
                            low.unsqueeze(2).to_broadcast([LIN, 2, GT * P]), ALU.subtract).then_inc(s_rows16, 1)
            v.wait_ge(s_srcl, 16)
            v.tensor_copy(srcl_s, srcl_i).then_inc(s_rows16, 1)

            v.wait_ge(s_src, 16)
            v.wait_ge(s_typ, 16)
            v.scalar_tensor_tensor(out=idx_i, in0=srcs_i, scalar=float(RELS), in1=typ_i, op0=ALU.mult, op1=ALU.add)\
             .then_inc(s_idxc, 1)

            def split_bits(ints, part, bits):
                step(v.tensor_scalar(part, ints, P - 1, None, ALU.bitwise_and))
                step(v.tensor_copy(bits[:, 0], part))
                step(v.tensor_scalar(part, ints, 7, None, ALU.logical_shift_right))
                step(v.tensor_copy(bits[:, 1], part))

            split_bits(srcs_i, part_i, src_bits)
            step(v.tensor_copy(beforeb, early_w("before")))

            finish_stats(0)

            def turned_rows(k, u, s):
                v.wait_ge(turned, units_before(k, HROWS) + u + 3)
                if k == 0:
                    v.wait_ge(made0, UB * u + 1)
                else:
                    v.wait_ge(made, units_before(k, (1, 2)) + u + 1)
                s = turn_slot(k, s)
                v.tensor_copy(hT[:, s].rearrange("p b f -> p (b f)"), BANK[2 + s][:, :]).then_inc(ht_ok, 1)

            def half_rows0(u, s):
                for b in range(UB):
                    v.wait_ge(made0, UB * u + b + UB + 2)
                    v.wait_ge(row_out[b % 2], stored(0, 0) + 16 * (UB // 2 * u + b // 2))
                    v.tensor_copy(t0row[:, b % 2, 512:1024], BANK[5 + 2 * (b % 2)][:, :]).then_inc(row0_v, 1)

            ahead(v, 1, lambda u, s: turned_rows(0, u, s), half_rows0)
            v.wait_ge(s_ewt, 16)

            def begin_edges(i, n):
                v.wait_ge(vec_in, 16 * (n + 1))
                v.tensor_tensor(vsq, vbuf, vbuf, ALU.mult).then_inc(y_step, 1)
                v.wait_ge(y_step, 4 * n + 1)
                v.tensor_reduce(vlen, vsq, AX.X, ALU.add).then_inc(y_step, 1)
                v.wait_ge(y_step, 4 * n + 2)
                v.tensor_scalar(vlen, vlen, 1.3e-35, None, ALU.max).then_inc(len_ok, 1)
                v.wait_ge(rad_in, 16 * (n + 1))
                v.wait_ge(emb_out, 16 * n + 1)
                v.tensor_scalar(ebuf, rbuf, 0.0, 1.0, ALU.max, ALU.min).then_inc(clip_ok, 1)

            def finish_edges(i, n):
                v.wait_ge(root_ok, n + 1)
                v.tensor_scalar(vlen, vlen, 1e-12, None, ALU.add).then_inc(y_step, 1)
                v.wait_ge(y_step, 4 * n + 3)
                v.reciprocal(vlen, vlen).then_inc(y_step, 1)
                v.wait_ge(y_step, 4 * n + 4)
                v.scalar_tensor_tensor(out=vbuf, in0=vbuf, scalar=3.0 ** 0.5,
                                       in1=vlen.unsqueeze(2).to_broadcast([P, IT, 3]), op0=ALU.mult, op1=ALU.mult)\
                 .then_inc(y_ok, 1)
                v.wait_ge(exp_ok, n + 1)
                v.scalar_tensor_tensor(out=ebuf, in0=rbuf, scalar=1.0, in1=ebuf, op0=ALU.is_le, op1=ALU.mult)\
                 .then_inc(emb_ok, 1)

            def group_tiles(array, i, j):
                return array[:, ds(GT * (4 * i + j), GT)]

            def select(p, i, j, g):
                if p == 1:
                    v.wait_ge(aggs[p], 2 * g + 2)
                else:
                    v.wait_ge(aggs[p], g + 3)
                at = sel[:, j % 2]
                eq = v.tensor_tensor(at, IOB[:, 0:W].unsqueeze(1).to_broadcast([P, GT, W]),
                                     group_tiles(DREL, i, j).unsqueeze(2).to_broadcast([P, GT, W]), ALU.is_equal)
                if p == 0:
                    eq.then_inc(s_wsel, 1)
                    v.wait_ge(s_wsel, g + 1)
                    eq = v.tensor_tensor(at, at, group_tiles(ew_t, i, j).unsqueeze(2).to_broadcast([P, GT, W]), ALU.mult)
                eq.then_inc(sel_ready[p], 1)

            def accumulate(p, i, j, g):
                start = v.value_load(ADDR[0:1, ds(4 * i + j, 1)], min_val=0, max_val=ADDR_MAX)
                v.wait_ge(aggs[p], 2 * g + 6 if p == 1 else g + 5)
                v.wait_ge(acc_done[p], g + 2)
                if p == 1:
                    part = A1[:, ds(start, W)]
                    v.tensor_tensor(part, part, BANK[6 + j % 2][:, 0:W], ALU.add)
                part = A0[:, ds(start, W)]
                v.tensor_tensor(part, part, BANK[4 + j % 2][:, 0:W], ALU.add).then_inc(acc_done[p], 1)

            def move_windows(p, r):
                v.wait_ge(sel_ready[p], GROUPS * (r + 1))
                v.tensor_scalar(DREL[:, :], DREL[:, :], float(W), None, ALU.subtract).then_inc(moved[p], 1)
                v.tensor_scalar(ADDR[:, :], ADDR[:, :], float(W), float(ADDR_MAX), ALU.add, ALU.min).then_inc(moved[p], 1)

            def reset_windows(p):
                v.wait_ge(moved[p], 2 * nr + 1)
                step(v.tensor_scalar(DREL[:, :], DREL[:, :], NRW[:, 0:1], None, ALU.add))
                step(v.tensor_copy(ADDR[:, :], ADDR0[:, :]))

            def plain_pass(p):
                deg = DEG[:, COUNTED.index(p)] if p in COUNTED else None
                for s in range(2):
                    v.wait_ge(row_out[s], stored(p + 1, s))
                v.wait_ge(s_zero0[p], 1)
                with v.Fori(0, nr) as r:
                    v.wait_ge(moved[p], 2 * r + 1)
                    apart(v)
                    if p in COUNTED:
                        before = COUNTED.index(p) * nr
                        v.wait_ge(deg_ok, GROUPS * (before + r) + 1)
                        apart(v)
                        v.memset(deg, 0.0).then_inc(deg_zero, 1)
                        v.wait_ge(deg_zero, before + r + 1)
                        apart(v)
                    with v.Fori(0, ITS) as i:
                        n = r * ITS + i
                        for j in range(IG):
                            g = 4 * n + j
                            if p == 0 and j == 1:
                                begin_edges(i, n)
                            if p == 0 and j == 3:
                                finish_edges(i, n)
                            if p in COUNTED:
                                bits = src_bits if p == 0 else dst_bits
                                c = COUNTED.index(p) * GROUPS * nr + g
                                v.wait_ge(hist_mm, c + 1)
                                for k, (at, wide) in enumerate(((0, P), (P, NB))):
                                    last = v.tensor_tensor(oh[:, :, at:at + wide],
                                                           IOB[:, 0:wide].unsqueeze(1).to_broadcast([P, GT, wide]),
                                                           group_tiles(bits[:, k], i, j).unsqueeze(2)
                                                           .to_broadcast([P, GT, wide]), ALU.is_equal)
                                last.then_inc(oh_ready, 1)
                            if p == 0:
                                v.wait_ge(srow0_in[j % 2], 16 * (2 * n + j // 2 + 1))
                                for t in range(GT):
                                    tile = GT * (4 * i + j) + t
                                    last = v.scalar_tensor_tensor(
                                        out=same0[:, t, :], in0=srow0[:, j % 2, P * t:P * t + P],
                                        scalar=srcs_i[:, ds(tile, 1)], in1=beforeb,
                                        op0=ALU.is_equal, op1=ALU.mult, accum_out=earlier[:, ds(tile, 1)])
                                last.then_inc(same0_ok, 1)
                            select(p, i, j, g)
                            if p in COUNTED:
                                v.wait_ge(hist_mm, c + 2)
                                v.wait_ge(deg_ok, c + 1)
                                v.tensor_tensor(deg, deg, BANK[6][:, 0:NB], ALU.add).then_inc(deg_ok, 1)
                            if j:
                                accumulate(p, i, j - 1, g - 1)
                        accumulate(p, i, IG - 1, 4 * n + IG - 1)
                    move_windows(p, r)
                reset_windows(p)

            def sums(k, rows, scale):
                slots = PARTS if k == 3 else 2

                def add(u, s):
                    some = rows[:, ds(UB * u, UB), :]
                    if k == 3:
                        x_rows = X[:, ds(UB * u, UB), :]
                        v.tensor_tensor(x_rows, x_rows, res("beta").unsqueeze(1).to_broadcast([P, UB, FEAT]), ALU.add)
                    v.wait_ge(projected, units_before(k, SUMS) + u + 3)
                    v.scalar_tensor_tensor(out=some, in0=BANK[slot(k, s)][:, :].rearrange("p (b f) -> p b f", b=UB),
                                           scalar=scale, in1=some, op0=ALU.mult, op1=ALU.add).then_inc(added, 1)

                def statistics(u, s):
                    v.wait_ge(added, units_before(k, SUMS) + u + 3)
                    row_stats(lambda b: rows[:, ds(UB * u + b, 1), :].rearrange("p b f -> p (b f)"), UB * u)

                ahead(v, 1, add, statistics, slots)

            plain_pass(0)

            def clip_degrees(k):
                v.wait_ge(deg_ok, (k + 1) * (GROUPS * nr) + 1)
                v.tensor_scalar(DEG[:, k], DEG[:, k], 1.0, None, ALU.max).then_inc(s_deg, 1)

            def invert_roots(k):
                v.wait_ge(s_degr, k + 1)
                step(v.reciprocal(DEG[:, k], DEG[:, k]))

            v.wait_ge(same0_ok, GROUPS * nr + 2)
            step(v.tensor_scalar(sidx_f, res("rowno").to_broadcast([P, TILES]), float(SPARE), None, ALU.add))
            step(v.tensor_tensor(sidx_f, sidx_f, srcs_i, ALU.subtract))
            step(v.scalar_tensor_tensor(out=sidx_f, in0=earlier, scalar=1.0, in1=sidx_f, op0=ALU.min, op1=ALU.mult))
            v.tensor_tensor(sidx_i, sidx_f, srcs_i, ALU.add).then_inc(s_sidx, 1)

            clip_degrees(0)
            sums(1, X, 1.0)
            invert_roots(0)
            finish_stats(1)
            A1r = A1[:, :].rearrange("p (b f) -> p b f", f=FEAT)

            def table_rows(k):
                def made_rows(u, s):
                    v.wait_ge(made, units_before(k, (1, 2)) + u + 3)
                    used = 8 * (u - s)
                    s = slot(k, s)
                    v.wait_ge(row_out[s], stored(k, s) + used)
                    made_v = BANK[4 + s][:, :].rearrange("p (b f) -> p b f", b=UB)
                    if k == 1:
                        ins = v.tensor_scalar(trow[:, s], made_v, float(MUL) ** -0.5, None, ALU.mult)
                    else:
                        ins = v.tensor_tensor(trow[:, s], made_v, res("bl").unsqueeze(1).to_broadcast([P, UB, FEAT]), ALU.add)
                    ins.then_inc(row_ok, 1)

                ahead(v, 1, lambda u, s: turned_rows(k, u, s), made_rows)

            table_rows(1)

            def messages1(i, j, s, m):
                h, t0 = j // 2, GT * (j % 2) + 4 * s
                w4 = BANK[2 + s][:, :].rearrange("p (t k m) -> p t k m", t=4, k=4)
                rows = ring[:, j, 4 * s:4 * s + 4, :]
                sc = rows[:, :, 0:32]
                scal, ubuf = scals[:, s], ubufs[:, s]
                vv = rows[:, :, 32:128].rearrange("p t (c m) -> p t c m", c=3)
                M = msg1[:, s]
                m1 = M[:, :, 64:160].rearrange("p t (c m) -> p t c m", c=3)
                m2 = M[:, :, 160:256].rearrange("p t (c m) -> p t c m", c=3)
                y = ybuf[:, h, t0:t0 + 4, :].unsqueeze(3).to_broadcast([P, 4, 3, 32])
                v.wait_ge(aggs[1], m + 3)
                v.tensor_tensor(m2, vv, y, ALU.mult).then_inc(s_t, 1)
                v.wait_ge(w_mm, m + 2)
                v.tensor_tensor(scal, w4[:, :, 1], sc, ALU.mult).then_inc(s_scal, 1)
                v.wait_ge(s_t, m + 1)
                v.tensor_tensor(ubuf, m2[:, :, 0], m2[:, :, 1], ALU.add).then_inc(s_u, 1)
                v.tensor_tensor(M[:, :, 0:32], w4[:, :, 0], sc, ALU.mult)
                v.wait_ge(s_u, 2 * m + 1)
                v.tensor_tensor(ubuf, ubuf, m2[:, :, 2], ALU.add).then_inc(s_u, 1)
                v.wait_ge(s_scal, m + 1)
                v.tensor_tensor(m1, scal.unsqueeze(2).to_broadcast([P, 4, 3, 32]), y, ALU.mult)
                v.wait_ge(s_u, 2 * m + 2)
                v.tensor_tensor(M[:, :, 32:64], w4[:, :, 3], ubuf, ALU.mult)
                v.tensor_tensor(m2, vv, w4[:, :, 2].unsqueeze(2).to_broadcast([P, 4, 3, 32]), ALU.mult).then_inc(msg_ok[0], 1)

            for s in range(2):
                v.wait_ge(row_out[s], stored(2, s))
            v.memset(emb[64:128, :], 0.0).then_inc(emb_pad, 1)
            v.wait_ge(s_zero0[1], 1)
            v.wait_ge(s_zero1, 1)
            with v.Fori(0, nr) as r:
                v.wait_ge(moved[1], 2 * r + 1)
                apart(v)
                def turn1(i, is_first):
                    n = r * ITS + i
                    for j in range(IG):
                        g = 4 * n + j
                        if j % 2 == 0:
                            v.wait_ge(y_in[j // 2], 16 * (n + 1))
                        select(1, i, j, g)
                        v.wait_ge(rows_in[1][j], 16 * GT * (n + 1))
                        messages1(i, j, 0, 2 * g)
                        if j or not is_first:
                            accumulate(1, i, j - 1, g - 1)
                        messages1(i, j, 1, 2 * g + 1)

                turn1(0, True)
                with v.Fori(0, ITS - 1) as i:
                    turn1(i + 1, False)
                accumulate(1, ITS - 1, IG - 1, (r + 1) * GROUPS - 1)
                move_windows(1, r)
            reset_windows(1)

            sums(2, X, 1.0 / (8.0 * 16.0))
            finish_stats(2)
            table_rows(2)

            v.wait_ge(s_zero0[2], 1)

            def pick_rows(n, j):
                g = 4 * n + j
                v.wait_ge(rbf_in[j % 2], 64 * (2 * n + j // 2 + 1))
                v.wait_ge(rows_mm, 2 * g + 2)
                v.tensor_scalar(pick[0:W, j % 2], drow[0:W, j % 2], NODE[0:W, 0:1], None, ALU.is_equal).then_inc(pick_ok, 1)

            def same_source(n, j):
                g = 4 * n + j
                if j % 2 == 0:
                    v.wait_ge(srcc_in[j // 2], 16 * (n + 1))
                v.wait_ge(comb_mm, 2 * g + 2)
                for t in range(GT):
                    c = GT * j + t
                    last = v.tensor_scalar(same[:, j % 2, t, :], srow[:, j % 2, P * t:P * t + P], srcc[:, c:c + 1], None,
                                           ALU.is_equal)
                last.then_inc(same_ok, 1)

            with v.Fori(0, nr) as r:
                v.wait_ge(moved[2], 2 * r + 1)
                apart(v)
                def turn2(n, is_last):
                    for j in range(IG):
                        after = (n, j + 1) if j + 1 < IG else (n + 1, 0)
                        more = j + 1 < IG or not is_last
                        for s in range(2):
                            if s == 1 and more:
                                pick_rows(*after)
                            m = 2 * (4 * n + j) + s
                            v.wait_ge(m_cp, m + 3)
                            v.wait_ge(rows_mm, m + 5)
                            v.wait_ge(comb_mm, m + 3)
                            v.tensor_tensor(msg2[:, s].rearrange("p t f -> p (t f)"), mout[:, s], BANK[4 + s][:, :],
                                            ALU.mult).then_inc(msg_ok[1], 1)
                            if s == 1 and more:
                                same_source(*after)

                n0 = r * ITS
                pick_rows(n0, 0)
                same_source(n0, 0)
                with v.Fori(0, ITS - 1) as i:
                    turn2(n0 + i, False)
                turn2(n0 + ITS - 1, True)
                v.wait_ge(pick_ok, GROUPS * (r + 1))
                v.tensor_scalar(NODE[:, :], NODE[:, :], float(W), None, ALU.add).then_inc(moved[2], 1)
                v.tensor_scalar(ADDR[:, :], ADDR[:, :], float(W), float(ADDR_MAX), ALU.add, ALU.min).then_inc(moved[2], 1)
            v.wait_ge(moved[2], 2 * nr + 1)
            step(v.tensor_copy(ADDR[:, :], ADDR0[:, :]))
            v.wait_ge(s_dsts, 16)
            v.wait_ge(zero_out, zeroed(nr))
            apart(v)
            split_bits(dsts_i, dpart_i, dst_bits)

            v.wait_ge(keep_ok, UNITS)
            sums(3, A1r, 1.0)
            finish_stats(3)

            def scale_norm(u, s):
                v.wait_ge(normed, u + 1)
                v.tensor_tensor(hT[:, s], A1r[:, ds(UB * u, UB), :], res("gamma").unsqueeze(1).to_broadcast([P, UB, FEAT]),
                                ALU.mult).then_inc(scaled, 1)

            def add_norm(u, s):
                some = X[:, ds(UB * u, UB), :]
                v.wait_ge(scaled, u + 1)
                v.tensor_tensor(some, some, hT[:, s], ALU.add).then_inc(affine, 1)
                v.wait_ge(affine, u + 1)
                row_stats(lambda b: x_block(UB * u + b), UB * u)

            ahead(v, 1, scale_norm, add_norm)
            finish_stats(4)

            def rows3(u, s):
                used = 8 * (u - s)
                s = slot(3, s)
                v.wait_ge(normed, UNITS + u + 1)
                v.wait_ge(row_out[s], stored(3, s) + used)
                v.tensor_tensor(trow[:, s], A1r[:, ds(UB * u, UB), :],
                                DEG[:, 0, ds(UB * u, UB)].unsqueeze(2).to_broadcast([P, UB, FEAT]), ALU.mult)\
                 .then_inc(row_ok, 1)

            each_unit(v, rows3)

            def conv_rows(k, bias):
                def rows(u, s):
                    used = 8 * (u - s)
                    s = slot(k, s)
                    t = hT[:, s]
                    v.wait_ge(projected, units_before(k, SUMS) + u + 3)
                    v.tensor_tensor(t, BANK[s][:, :].rearrange("p (b f) -> p b f", b=UB),
                                    DEG[:, 1, ds(UB * u, UB)].unsqueeze(2).to_broadcast([P, UB, FEAT]), ALU.mult)\
                     .then_inc(added, 1)
                    v.wait_ge(added, units_before(k, SUMS) + u + 3)
                    v.tensor_tensor(t, t, res(bias).unsqueeze(1).to_broadcast([P, UB, FEAT]), ALU.add).then_inc(fin, 1)
                    if k == 4:
                        v.wait_ge(fin, 2 * u + 1)
                        v.scalar_tensor_tensor(out=t, in0=t, scalar=0.0, in1=A1r[:, ds(UB * u, UB), :], op0=ALU.max, op1=ALU.add)\
                         .then_inc(fin, 1)
                        v.wait_ge(fin, 2 * u + 2)
                        v.wait_ge(row_out[s], stored(k, s) + used)
                        v.tensor_tensor(trow[:, s], t, DEG[:, 0, ds(UB * u, UB)].unsqueeze(2).to_broadcast([P, UB, FEAT]),
                                        ALU.mult).then_inc(row_ok, 1)
                    else:
                        v.wait_ge(fin, 2 * UNITS + u + 1)
                        v.wait_ge(row_out[s], stored(k, s) + used)
                        v.scalar_tensor_tensor(out=trow[:, s], in0=t, scalar=0.0, in1=X[:, ds(UB * u, UB), :],
                                               op0=ALU.max, op1=ALU.add).then_inc(row_ok, 1)
                return rows

            plain_pass(3)
            clip_degrees(1)
            invert_roots(1)
            each_unit(v, conv_rows(4, "gb1"))
            step(v.scalar_tensor_tensor(out=X[:, :, :], in0=A1r, scalar=2.0, in1=X[:, :, :], op0=ALU.mult, op1=ALU.add))
            plain_pass(4)
            each_unit(v, conv_rows(5, "gb2"))

        @block.tensor
        def _(pe):
            mm = nc.tensor.matmul
            ident = res("ident")
            pe.wait_ge(s_early, 16)
            mm(BANK[7][:, 0:128], early_w("w0"), early_w("w0t"), start=True, stop=True).then_inc(s_cmm, 1)
            nr = rounds(pe)
            pe.wait_ge(s_res, 16)
            pe.wait_ge(s_cok, 1)

            def turn(k, u, s):
                u = units_before(k, HROWS) + u
                s = turn_slot(k, s)
                pe.wait_ge(hrow_ok, u + 3)
                pe.wait_ge(ht_ok, u + 1)
                for b in range(UB):
                    last = nc.tensor.transpose(BANK[2 + s][:, 128 * b:128 * b + 128], hrow[:, s, b, :], ident)
                last.then_inc(turned, 1)

            def relations(u, s):
                pe.wait_ge(ht_ok, u + 3)
                for b in range(UB):
                    k = 4 + 2 * (b % 2)
                    pe.wait_ge(row0_a, UB * u + b + 1)
                    pe.wait_ge(row0_v, UB * u + b + 1)
                    mm(BANK[k][:, :], hT[:, s, b, :], wall[:, 0:512], start=True, stop=True)
                    mm(BANK[k + 1][:, :], hT[:, s, b, :], wall[:, 512:1024], start=True, stop=True).then_inc(made0, 1)

            ahead(pe, 1, lambda u, s: turn(0, u, s), relations)
            pe.wait_ge(row0_a, NB + 2)
            pe.wait_ge(row0_v, NB + 2)

            def plain_pass(p):
                with pe.Fori(0, nr) as r:
                    with pe.Fori(0, ITS) as i:
                        n = r * ITS + i
                        for j in range(IG):
                            g = 4 * n + j
                            if p in COUNTED:
                                c = COUNTED.index(p) * GROUPS * nr + g
                                pe.wait_ge(oh_ready, c + 1)
                                pe.wait_ge(deg_ok, c + 1)
                                for t in range(GT):
                                    last = mm(BANK[6][:, 0:NB], oh[:, t, 0:P], oh[:, t, P:P + NB],
                                              start=(t == 0), stop=(t == GT - 1))
                                last.then_inc(hist_mm, 1)
                            pe.wait_ge(sel_ready[p], g + 1)
                            pe.wait_ge(acc_done[p], g + 1)
                            pe.wait_ge(rows_in[p][j], 16 * GT * (n + 1))
                            for t in range(GT):
                                last = mm(BANK[4 + j % 2][:, 0:W], ring[:, j, t, :], sel[:, j % 2, t, :],
                                          start=(t == 0), stop=(t == GT - 1))
                            last.then_inc(aggs[p], 1)

            def project(k):
                def unit(u, s):
                    s = slot(k, s)
                    pe.wait_ge(added, units_before(k, SUMS) + u + 1)
                    pe.wait_ge(staged, units_before(k, STAGED) + u + 3)
                    for b in range(UB):
                        to = BANK[s][:, P * b:P * b + P]
                        half = stage[:, s, 0, P * b:P * b + P]
                        if k == 1:
                            last = nc.tensor.transpose(to, half, ident)
                        elif k == 2:
                            mm(to, half, res("woa"), start=True, stop=False)
                            last = mm(to, stage[:, s, 1, P * b:P * b + P], res("wob"), start=False, stop=True)
                        else:
                            last = mm(to, half, res("g1" if k == 4 else "g2"), start=True, stop=True)
                    last.then_inc(projected, 1)

                each_unit(pe, unit)

            def table(k, weights):
                def product(u, s):
                    pe.wait_ge(ht_ok, units_before(k, HROWS) + u + 3)
                    pe.wait_ge(row_ok, units_before(k, ROWS) + u + 1)
                    for b in range(UB):
                        last = mm(BANK[4 + slot(k, s)][:, P * b:P * b + P], hT[:, turn_slot(k, s), b, :], weights,
                                  start=True, stop=True)
                    last.then_inc(made, 1)

                ahead(pe, 1, lambda u, s: turn(k, u, s), product)

            plain_pass(0)
            project(1)
            table(1, res("wup"))

            def first_hidden(n, j):
                g = 4 * n + j
                if j == 0:
                    pe.wait_ge(emb_in, 16 * (n + 1))
                pe.wait_ge(h1_ok, g + 1)
                mm(BANK[0][:, :], res("ew")[:, 128 * j:128 * j + 128], emb, start=True, stop=True).then_inc(h1_mm, 1)

            def second_hidden(g):
                pe.wait_ge(h1_ok, g + 2)
                pe.wait_ge(h2_ok, g + 1)
                mm(BANK[1][:, :], res("w1b"), h1, start=True, stop=True).then_inc(h2_mm, 1)

            def bias_mm(to, k):
                return mm(to, ONES[:, :], B2S[:, k, :], start=False, stop=True)

            def weights1(g, s):
                m = 2 * g + s
                if s == 0:
                    pe.wait_ge(h2_ok, g + 2)
                pe.wait_ge(msg_ok[0], m + 7)
                for t in range(4):
                    to = BANK[2 + s][:, 128 * t:128 * t + 128]
                    mm(to, h2[:, 128 * t:128 * t + 128], res("w2p")[:, 128 * s:128 * s + 128], start=True, stop=False)
                    last = bias_mm(to, 0)
                last.then_inc(w_mm, 1)

            def sums1(j, g, s):
                m = 2 * g + s
                if s == 0:
                    pe.wait_ge(sel_ready[1], g + 1)
                    pe.wait_ge(acc_done[1], g + 1)
                pe.wait_ge(msg_ok[0], m + 9)
                for a in range(2):
                    for t in range(4):
                        last = mm(BANK[4 + 2 * a + j % 2][:, 0:W], msg1[:, s, t, 128 * a:128 * a + 128],
                                  sel[:, j % 2, 4 * s + t, :], start=(s == 0 and t == 0), stop=(s == 1 and t == 3))
                last.then_inc(aggs[1], 1)

            pe.wait_ge(emb_pad, 1)
            with pe.Fori(0, nr) as r:
                def turn1(n, is_last):
                    for j in range(IG):
                        g = 4 * n + j
                        more = j + 1 < IG or not is_last
                        if more:
                            second_hidden(g + 1)
                        for s in range(2):
                            sums1(j, g, s)
                            if more:
                                weights1(g + 1, s)
                            if s == 0 and (j + 2 < IG or not is_last):
                                first_hidden(n + (j + 2) // IG, (j + 2) % IG)

                n0 = r * ITS
                first_hidden(n0, 0)
                second_hidden(4 * n0)
                first_hidden(n0, 1)
                weights1(4 * n0, 0)
                weights1(4 * n0, 1)
                with pe.Fori(0, ITS - 1) as i:
                    turn1(n0 + i, False)
                turn1(n0 + ITS - 1, True)

            project(2)
            table(2, res("wlt"))

            def inner2(n, q):
                m, j, s = 8 * n + q, q // 2, q % 2
                if s == 0:
                    pe.wait_ge(rbf_in[j % 2], 64 * (2 * n + j // 2 + 1))
                pe.wait_ge(c_ok, m + 1)
                mm(BANK[s][:, :], CW[:, :], rbf_t[:, j % 2, 512 * s:512 * s + 512], start=True, stop=True).then_inc(c_mm, 1)

            def outer2(n, q):
                m, s = 8 * n + q, q % 2
                pe.wait_ge(c_ok, m + 3)
                pe.wait_ge(m_cp, m + 1)
                for t in range(4):
                    to = BANK[2 + s][:, 128 * t:128 * t + 128]
                    mm(to, hs2[:, s, 128 * t:128 * t + 128], res("w2t"), start=True, stop=False)
                    last = bias_mm(to, 1)
                last.then_inc(m_mm, 1)

            def rows2(n, q):
                m, j, s = 8 * n + q, q // 2, q % 2
                if s == 0:
                    pe.wait_ge(pick_ok, 4 * n + j + 1)
                pe.wait_ge(msg_ok[1], m + 7)
                for t in range(4):
                    last = mm(BANK[4 + s][:, 128 * t:128 * t + 128], pick[:, j % 2, 128 * (4 * s + t):128 * (4 * s + t + 1)],
                              twin[:, j % 2, :], start=True, stop=True)
                last.then_inc(rows_mm, 1)

            def equal2(n, q):
                m, j, s = 8 * n + q, q // 2, q % 2
                if s == 0:
                    pe.wait_ge(same_ok, 4 * n + j + 4)
                pe.wait_ge(scat_ok, m + 1)
                pe.wait_ge(msg_ok[1], m + 9)
                for t in range(4):
                    last = mm(BANK[6 + s][:, 128 * t:128 * t + 128], same[:, j % 2, 4 * s + t, :], msg2[:, s, t, :],
                              start=True, stop=True)
                last.then_inc(comb_mm, 1)

            with pe.Fori(0, nr) as r:
                def turn2(n, is_last):
                    for q in range(2 * IG):
                        after = (n, q + 1) if q + 1 < 2 * IG else (n + 1, 0)
                        more = q + 1 < 2 * IG or not is_last
                        if more:
                            inner2(*after)
                        outer2(n, q)
                        if more:
                            rows2(*after)
                        if q:
                            equal2(n, q - 1)
                    equal2(n, 2 * IG - 1)

                n0 = r * ITS
                inner2(n0, 0)
                rows2(n0, 0)
                with pe.Fori(0, ITS - 1) as i:
                    turn2(n0 + i, False)
                turn2(n0 + ITS - 1, True)

            def add_parts(u, s):
                pe.wait_ge(added, units_before(3, SUMS) + u + 1)
                pe.wait_ge(part_in[s], 16 * COPIES // PARTS * (u - s + PARTS))
                for c in range(COPIES):
                    last = mm(BANK[s % 2][:, :], ident, parts[:, s, c, :], start=(c == 0), stop=(c == COPIES - 1))
                last.then_inc(projected, 1)

            each_unit(pe, add_parts, PARTS)
            plain_pass(3)
            project(4)
            plain_pass(4)
            project(5)


def _laid_out(inputs):
    import numpy as np
    a = {k: np.asarray(v) for k, v in inputs.items()}
    slots = TILES * P

    def edges(array, fill):
        full = np.full((slots,) + array.shape[1:], fill, array.dtype)
        full[:EDGES] = array
        return full.reshape((TILES, P) + array.shape[1:])

    x = np.zeros((NB, P, FEAT), np.float32)
    x.reshape(NP, FEAT)[:NODES] = a["x"]
    src = edges(a["src"].astype(np.int32), NODES).reshape(ITS, IT, P).transpose(0, 2, 1)
    dst = edges(a["dst"].astype(np.int32), NODES).T
    srcl = edges(a["src"].astype(np.int32), NODES).reshape(LIN, 2 * GT * P)
    dstl = edges(a["dst"].astype(np.int32), NODES).reshape(LIN, 2 * GT * P)
    etype = edges(a["edge_type_8"].astype(np.int32), 0).T
    eweight = edges(a["edge_weight"], 0).T
    evec = edges(a["edge_attr_3"], 0).transpose(1, 0, 2).reshape(P, 3 * TILES)
    rad = np.zeros((ITS, 2 * IG, 512), np.float32)
    rad.reshape(-1)[:EDGES] = a["edge_weight"]
    radii = np.repeat(rad, CENTERS, axis=1)
    rbf = edges(a["edge_attr_128"], 0).reshape(GROUPS, GT * P, FEAT).transpose(0, 2, 1)

    res = np.zeros((P, RES_N), np.float32)
    early = np.zeros((P, EARLY_N), np.float32)

    def put(name, value, rows=slice(None)):
        lo, hi = RES_AT[name]
        res[rows, lo:hi] = value

    w = np.zeros((P, 128), np.float32)
    w[:MUL, :MUL] = a["L1_gnn_W_up0"]
    for c in range(3):
        w[MUL + c::3, MUL + 32 * c:MUL + 32 * c + 32] = a["L1_gnn_W_up1"]
    put("wup", w)
    woa, wob = np.zeros((P, 128), np.float32), np.zeros((P, 128), np.float32)
    woa[0:64, 0:32] = a["L1_gnn_W_out0"]
    o1 = a["L1_gnn_W_out1"]
    woa[64:96, 32::3] = o1[0:32]
    woa[96:128, 33::3] = o1[0:32]
    wob[0:32, 34::3] = o1[0:32]
    for c in range(3):
        wob[32 + 32 * c:64 + 32 * c, 32 + c::3] = o1[32:64]
    put("woa", woa)
    put("wob", wob)
    ew = np.zeros((64, IG * 128), np.float32)
    for j in range(IG):
        for s in range(2):
            ew[16 * j + 8 * s:16 * j + 8 * s + 8, 128 * j + 64 * s:128 * j + 64 * s + 64] = a["L1_gnn_mlp_w0"]
    put("ew", ew, slice(0, 64))
    w = np.zeros((P, 128), np.float32)
    w[0:64, 0:64] = w[64:128, 64:128] = a["L1_gnn_mlp_w1"]
    put("w1b", w)
    w = np.zeros((P, 256), np.float32)
    w[0:64, 0:128] = w[64:128, 128:256] = a["L1_gnn_mlp_w2"]
    put("w2p", w)
    put("w2t", a["L2_gnn_W2"].T)
    put("wlt", a["L2_gnn_Wl"].T)
    for name, key in (("bl", "L2_gnn_bl"), ("gamma", "L2_gnn_gamma"), ("beta", "L2_gnn_beta"),
                      ("gb1", "L3_gnn_b1"), ("gb2", "L3_gnn_b2"), ("g1", "L3_gnn_W1"), ("g2", "L3_gnn_W2")):
        put(name, a[key])
    put("mb0", np.concatenate([a["L1_gnn_mlp_b0"]] * 2)[:, None])
    put("mb1", np.concatenate([a["L1_gnn_mlp_b1"]] * 2)[:, None])
    put("cb0", a["L2_gnn_b0"][:, None])
    put("ident", np.eye(P, dtype=np.float32))
    put("ncen", -(np.arange(P) % CENTERS).astype(np.float32)[:, None])
    put("rowm", np.eye(3, dtype=np.float32), slice(0, 3))
    put("rowno", np.arange(P, dtype=np.float32)[:, None])
    put("eps", EPS)

    def put_early(name, value):
        lo, hi = EARLY_AT[name]
        early[:, lo:hi] = value

    put_early("bases", a["L0_gnn_bases"].transpose(1, 0, 2).reshape(P, -1))
    put_early("wcomp", a["L0_gnn_w_comp"].reshape(1, -1))
    put_early("w0", a["L2_gnn_W0"])
    put_early("w0t", a["L2_gnn_W0"].T)
    put_early("b2a", a["L1_gnn_mlp_b2"])
    put_early("b2b", a["L2_gnn_b2"])
    put_early("iota", np.arange(128, dtype=np.float32))
    put_early("before", np.tri(P, k=-1, dtype=np.float32))
    put_early("kvec", W * np.arange(1, KV + 1, dtype=np.float32))
    out = dict(x=x, src=src, dst=dst, srcl=srcl, dstl=dstl, etype=etype, eweight=eweight, radii=radii, evec=evec, rbf=rbf,
               resident=res, early=early)
    return {k: np.ascontiguousarray(v) for k, v in out.items()}


def kernel(**inputs):
    import numpy as _np
    import concourse.bacc as _bacc
    from concourse import mybir as _mybir
    from concourse.bass_utils import run_bass_kernel_spmd as _run

    nc = _bacc.Bacc("TRN2", target_bir_lowering=False, num_devices=1)
    laid = _laid_out(inputs)
    args = [nc.dram_tensor(f"in_{k}", v.shape, _mybir.dt.from_np(v.dtype), kind="ExternalInput").ap()
            for k, v in laid.items()]
    args.append(nc.dram_tensor("out_0", (NP, FEAT), _mybir.dt.float32, kind="ExternalOutput").ap())
    gnn_kernel(nc, *args)
    r = _run(nc, [{f"in_{k}": v for k, v in laid.items()}], core_ids=[0])
    return _np.asarray(r.results[0]["out_0"])[:NODES]
```
